# Optimizing a Trainium2 kernel written in Bass

```python
import numpy as np
import jax
import jax.numpy as jnp

def _softmax(x, axis=-1):
    return jax.nn.softmax(x, axis=axis)

def _gelu(x):
    return jax.nn.gelu(x, approximate=True)

def _silu(x):
    return jax.nn.silu(x)

def _sigmoid(x):
    return jax.nn.sigmoid(x)

def _layernorm(x, axis=-1, eps=1e-05):
    m = jnp.mean(x, axis=axis, keepdims=True)
    v = jnp.var(x, axis=axis, keepdims=True)
    return (x - m) / jnp.sqrt(v + eps)

def _scatter_add(tgt, idx, src, axis=0):
    return tgt.at[idx].add(src)

def _segment_sum(src, seg, n):
    return jax.ops.segment_sum(src, seg, n)
kernel_name = 'mk_metaformer_d1_conv_nhwc256_r4_212c16'

def setup_inputs(seed: int=0):
    np.random.seed(seed)
    _w = jnp.asarray

    def _rec_inputs():
        import jax
        import jax.numpy as jnp
        _gk = jax.random.key(seed)
        x = 7.22e-05 + 1 * jax.random.normal(jax.random.fold_in(_gk, 1), (8, 16, 16, 64), jnp.float32)
        return x
    x = _rec_inputs()

    def _L0_conv_setup():
        import jax, jax.numpy as jnp
        import numpy as np
        B, H, W, C = (8, 16, 16, 64)
        G, K = (8, 3)
        GC = C // G
        K2 = K * K
        KD = 3
        OFFSET_SCALE = 1.0
        PAD = (K - 1) // 2
        EPS = 1e-06

        def _bilinear_gather(xg, px, py, Hp, Wp):
            x0 = jnp.floor(px)
            y0 = jnp.floor(py)
            wx1 = px - x0
            wy1 = py - y0
            x0i = x0.astype(jnp.int32)
            y0i = y0.astype(jnp.int32)

            def corner(xi, yi, wgt):
                valid = (xi >= 0) & (xi < Wp) & (yi >= 0) & (yi < Hp)
                idx = jnp.clip(yi, 0, Hp - 1) * Wp + jnp.clip(xi, 0, Wp - 1)
                v = jnp.take_along_axis(xg, idx[..., None], axis=2)
                return v * (wgt * valid)[..., None]
            return corner(x0i, y0i, (1 - wx1) * (1 - wy1)) + corner(x0i + 1, y0i, wx1 * (1 - wy1)) + corner(x0i, y0i + 1, (1 - wx1) * wy1) + corner(x0i + 1, y0i + 1, wx1 * wy1)
        key = jax.random.key(seed)
        ks = jax.random.split(key, 8)

        def r(k, shp, s):
            return jax.random.normal(k, shp, jnp.float32) * s
        return {'inputs': jax.random.normal(ks[0], (B, H, W, C), jnp.float32), 'w_in': r(ks[1], (C, C), 0.02), 'b_in': jnp.zeros((C,), jnp.float32), 'dw_kernel': r(ks[2], (KD, KD, 1, C), 0.1), 'dw_bias': jnp.zeros((C,), jnp.float32), 'ln_gamma': jnp.ones((C,), jnp.float32), 'ln_beta': jnp.zeros((C,), jnp.float32), 'w_off': r(ks[3], (C, 2 * G * K2), 0.01), 'b_off': jnp.zeros((2 * G * K2,), jnp.float32), 'w_mask': r(ks[4], (C, G * K2), 0.01), 'b_mask': jnp.zeros((G * K2,), jnp.float32), 'w_out': r(ks[5], (C, C), 0.02), 'b_out': jnp.zeros((C,), jnp.float32)}
    _L0_conv_all = _L0_conv_setup()
    _L0_conv_in = {k: v for k, v in _L0_conv_all.items() if k in ('w_in', 'b_in', 'dw_kernel', 'dw_bias', 'ln_gamma', 'ln_beta', 'w_off', 'b_off', 'w_mask', 'b_mask', 'w_out', 'b_out')}
    del _L0_conv_all

    def _L0_ffn_setup():
        import jax, jax.numpy as jnp
        import numpy as np
        TOP_K = 2
        LN_EPS = 1e-05
        key = jax.random.key(seed)
        ks = jax.random.split(key, 8)
        B, S, D, E, H = (16, 256, 64, 8, 256)
        x = jax.random.normal(ks[0], (B, S, D), dtype=jnp.float32)
        Wr = jax.random.normal(ks[1], (D, E), dtype=jnp.float32) * 0.1
        br = jnp.zeros((E,), dtype=jnp.float32)
        ln_g = jnp.ones((E, D), dtype=jnp.float32)
        ln_b = jnp.zeros((E, D), dtype=jnp.float32)
        W1 = jax.random.normal(ks[2], (E, D, H), dtype=jnp.float32) * (1.0 / np.sqrt(D))
        b1 = jnp.zeros((E, H), dtype=jnp.float32)
        W2 = jax.random.normal(ks[3], (E, H, D), dtype=jnp.float32) * (1.0 / np.sqrt(H))
        b2 = jnp.zeros((E, D), dtype=jnp.float32)
        return {'x': x, 'Wr': Wr, 'br': br, 'ln_g': ln_g, 'ln_b': ln_b, 'W1': W1, 'b1': b1, 'W2': W2, 'b2': b2}
    _L0_ffn_all = _L0_ffn_setup()
    _L0_ffn_in = {k: v for k, v in _L0_ffn_all.items() if k in ('Wr', 'br', 'ln_g', 'ln_b', 'W1', 'b1', 'W2', 'b2')}
    del _L0_ffn_all
    return {'x': x, 'L0_conv_w_in': _L0_conv_in['w_in'], 'L0_conv_b_in': _L0_conv_in['b_in'], 'L0_conv_dw_kernel': _L0_conv_in['dw_kernel'], 'L0_conv_dw_bias': _L0_conv_in['dw_bias'], 'L0_conv_ln_gamma': _L0_conv_in['ln_gamma'], 'L0_conv_ln_beta': _L0_conv_in['ln_beta'], 'L0_conv_w_off': _L0_conv_in['w_off'], 'L0_conv_b_off': _L0_conv_in['b_off'], 'L0_conv_w_mask': _L0_conv_in['w_mask'], 'L0_conv_b_mask': _L0_conv_in['b_mask'], 'L0_conv_w_out': _L0_conv_in['w_out'], 'L0_conv_b_out': _L0_conv_in['b_out'], 'L0_ffn_Wr': _L0_ffn_in['Wr'], 'L0_ffn_br': _L0_ffn_in['br'], 'L0_ffn_ln_g': _L0_ffn_in['ln_g'], 'L0_ffn_ln_b': _L0_ffn_in['ln_b'], 'L0_ffn_W1': _L0_ffn_in['W1'], 'L0_ffn_b1': _L0_ffn_in['b1'], 'L0_ffn_W2': _L0_ffn_in['W2'], 'L0_ffn_b2': _L0_ffn_in['b2']}

def reference(x, L0_conv_w_in, L0_conv_b_in, L0_conv_dw_kernel, L0_conv_dw_bias, L0_conv_ln_gamma, L0_conv_ln_beta, L0_conv_w_off, L0_conv_b_off, L0_conv_w_mask, L0_conv_b_mask, L0_conv_w_out, L0_conv_b_out, L0_ffn_Wr, L0_ffn_br, L0_ffn_ln_g, L0_ffn_ln_b, L0_ffn_W1, L0_ffn_b1, L0_ffn_W2, L0_ffn_b2):
    import jax
    import jax.numpy as jnp

    def _L0_conv_ref(inputs, w_in, b_in, dw_kernel, dw_bias, ln_gamma, ln_beta, w_off, b_off, w_mask, b_mask, w_out, b_out):
        import jax, jax.numpy as jnp
        import numpy as np
        B, H, W, C = (8, 16, 16, 64)
        G, K = (8, 3)
        GC = C // G
        K2 = K * K
        KD = 3
        OFFSET_SCALE = 1.0
        PAD = (K - 1) // 2
        EPS = 1e-06

        def _bilinear_gather(xg, px, py, Hp, Wp):
            x0 = jnp.floor(px)
            y0 = jnp.floor(py)
            wx1 = px - x0
            wy1 = py - y0
            x0i = x0.astype(jnp.int32)
            y0i = y0.astype(jnp.int32)

            def corner(xi, yi, wgt):
                valid = (xi >= 0) & (xi < Wp) & (yi >= 0) & (yi < Hp)
                idx = jnp.clip(yi, 0, Hp - 1) * Wp + jnp.clip(xi, 0, Wp - 1)
                v = jnp.take_along_axis(xg, idx[..., None], axis=2)
                return v * (wgt * valid)[..., None]
            return corner(x0i, y0i, (1 - wx1) * (1 - wy1)) + corner(x0i + 1, y0i, wx1 * (1 - wy1)) + corner(x0i, y0i + 1, (1 - wx1) * wy1) + corner(x0i + 1, y0i + 1, wx1 * wy1)
        x_proj = inputs @ w_in + b_in
        x1 = jax.lax.conv_general_dilated(inputs, dw_kernel, (1, 1), 'SAME', dimension_numbers=('NHWC', 'HWIO', 'NHWC'), feature_group_count=C) + dw_bias
        mu = jnp.mean(x1, -1, keepdims=True)
        var = jnp.mean(jnp.square(x1 - mu), -1, keepdims=True)
        x1 = (x1 - mu) * jax.lax.rsqrt(var + EPS) * ln_gamma + ln_beta
        x1 = jax.nn.gelu(x1, approximate=False)
        offset = (x1 @ w_off + b_off).reshape(B, H, W, G, K2, 2)
        mask = jax.nn.softmax((x1 @ w_mask + b_mask).reshape(B, H, W, G, K2), axis=-1)
        ky, kx = jnp.meshgrid(jnp.arange(K) - PAD, jnp.arange(K) - PAD, indexing='ij')
        kx = kx.reshape(-1).astype(jnp.float32)
        ky = ky.reshape(-1).astype(jnp.float32)
        px = (PAD + jnp.arange(W, dtype=jnp.float32))[None, None, :, None, None] + (kx + offset[..., 0]) * OFFSET_SCALE
        py = (PAD + jnp.arange(H, dtype=jnp.float32))[None, :, None, None, None] + (ky + offset[..., 1]) * OFFSET_SCALE
        Hp, Wp = (H + 2 * PAD, W + 2 * PAD)
        x_pad = jnp.pad(x_proj, ((0, 0), (PAD, PAD), (PAD, PAD), (0, 0)))
        xg = x_pad.reshape(B, Hp * Wp, G, GC).transpose(0, 2, 1, 3)
        N = H * W * K2
        pxf = px.transpose(0, 3, 1, 2, 4).reshape(B, G, N)
        pyf = py.transpose(0, 3, 1, 2, 4).reshape(B, G, N)
        samp = _bilinear_gather(xg, pxf, pyf, Hp, Wp).reshape(B, G, H, W, K2, GC)
        maskg = mask.transpose(0, 3, 1, 2, 4)
        out = jnp.sum(samp * maskg[..., None], axis=4)
        out = out.transpose(0, 2, 3, 1, 4).reshape(B, H, W, C)
        return out @ w_out + b_out

    def _L0_ffn_ref(x, Wr, br, ln_g, ln_b, W1, b1, W2, b2):
        import jax, jax.numpy as jnp
        import numpy as np
        TOP_K = 2
        LN_EPS = 1e-05
        B, S, D = x.shape
        N = B * S
        xt = x.reshape(N, D)
        logits = xt @ Wr + br
        probs = jax.nn.softmax(logits, axis=-1)
        top_p, top_idx = jax.lax.top_k(probs, TOP_K)
        weights = top_p / top_p.sum(axis=-1, keepdims=True)
        mu = xt.mean(axis=-1, keepdims=True)
        var = ((xt - mu) ** 2).mean(axis=-1, keepdims=True)
        xn = (xt - mu) * jax.lax.rsqrt(var + LN_EPS)
        xe = xn[None, :, :] * ln_g[:, None, :] + ln_b[:, None, :]
        h = jax.nn.gelu(jnp.einsum('end,edh->enh', xe, W1) + b1[:, None, :], approximate=False)
        y = jnp.einsum('enh,ehd->end', h, W2) + b2[:, None, :]
        y_tok = jnp.transpose(y, (1, 0, 2))
        sel = jnp.take_along_axis(y_tok, top_idx[:, :, None], axis=1)
        out = (weights[:, :, None] * sel).sum(axis=1)
        return out.reshape(B, S, D)

    def _gn(v, G=32, eps=1e-05):
        B_, H_, W_, C_ = v.shape
        g = v.reshape(B_, H_, W_, G, C_ // G)
        m = jnp.mean(g, axis=(1, 2, 4), keepdims=True)
        s = jnp.var(g, axis=(1, 2, 4), keepdims=True)
        return ((g - m) / jnp.sqrt(s + eps)).reshape(v.shape)

    def _ln_c(v, eps=1e-06):
        m = jnp.mean(v, axis=-1, keepdims=True)
        s = jnp.var(v, axis=-1, keepdims=True)
        return (v - m) / jnp.sqrt(s + eps)

    def _ln_t(v, eps=1e-05):
        m = jnp.mean(v, axis=-1, keepdims=True)
        s = jnp.var(v, axis=-1, keepdims=True)
        return (v - m) / jnp.sqrt(s + eps)

    def _to_tokens(v):
        B_, H_, W_, C_ = v.shape
        return v.reshape(B_, H_ * W_, C_)

    def _from_tokens(t, like):
        return t.reshape(like.shape)
    x = x + _L0_conv_ref(_ln_c(x), L0_conv_w_in, L0_conv_b_in, L0_conv_dw_kernel, L0_conv_dw_bias, L0_conv_ln_gamma, L0_conv_ln_beta, L0_conv_w_off, L0_conv_b_off, L0_conv_w_mask, L0_conv_b_mask, L0_conv_w_out, L0_conv_b_out)
    t = _to_tokens(x)
    t = t + _L0_ffn_ref(_ln_t(t), L0_ffn_Wr, L0_ffn_br, L0_ffn_ln_g, L0_ffn_ln_b, L0_ffn_W1, L0_ffn_b1, L0_ffn_W2, L0_ffn_b2)
    x = _from_tokens(t, x)
    return x

_drawn_inputs = setup_inputs


def setup_inputs(seed=0):
    import zlib

    import numpy as np

    out = dict(_drawn_inputs(seed))
    spreads = {'L0_conv_b_in': (0.0, 0.27),
     'L0_conv_dw_bias': (0.0, 2.0),
     'L0_conv_ln_gamma': (1.0, 0.6),
     'L0_conv_ln_beta': (0.0, 2.0),
     'L0_conv_b_off': (0.0, 2.0),
     'L0_conv_b_out': (0.0, 0.1),
     'L0_ffn_br': (0.0, 0.1),
     'L0_ffn_ln_g': (1.0, 0.2),
     'L0_ffn_ln_b': (0.0, 0.1),
     'L0_ffn_b1': (0.0, 0.1),
     'L0_ffn_b2': (0.0, 0.1)}
    factors = {'L0_conv_dw_kernel': 23.092, 'L0_conv_w_off': 22.519}
    for name, (base, spread) in spreads.items():
        noise = np.random.default_rng([zlib.crc32(name.encode()), seed]).standard_normal(out[name].shape)
        drawn = base * np.exp(spread * noise) if base else spread * noise
        out[name] = jnp.asarray(drawn.astype(out[name].dtype))
    for name, factor in factors.items():
        out[name] = (out[name] * factor).astype(out[name].dtype)
    return out
```

```python
from contextlib import ExitStack

import concourse.bass as bass
from concourse import mybir

F32 = mybir.dt.float32
F16 = mybir.dt.float16
ALU = mybir.AluOpType
ACT = mybir.ActivationFunctionType
AX = mybir.AxisListType

P = 128
B, H, W, C = 8, 16, 16, 64
G, K2 = 8, 9
GC = C // G
Q = G // 2
S = G * K2
TILES = B * H * W // P
PAIRS = B // 2
TP = TILES // PAIRS
HW = H * W
CELLS, LOC = 4, 5
KC = H * CELLS
NV = GC * 2 * LOC
NP = Q * K2
TR = 4
NG = NP // TR
PB = 6
NBK = NP // PB
WC = 3
SC = S // WC
E, HID = 8, 256
HC = HID // P
HR = 4
DR = 3
W_SCALE = 2.0 ** 8
V_SCALE = 2.0 ** 6
LINKS = 41

PE_IN = [18, 19, 20, 21, 22, 23, 24, 25] + [26, 27, 28, 29, 30, 31, 32, 33]
ACT_UNIT = [20, 20, 21, 22, 23, 24, 25, 26] + [27, 28, 29, 30, 31, 32, 33, 34]
PE_OUT = [21, 21, 22, 23, 24, 25, 26, 27] + [30, 30, 31, 31, 32, 33, 34, 35]


def first(i):
    return isinstance(i, int) and i == 0


def last(i):
    return isinstance(i, int) and i == PAIRS - 1


CI = {}
_at = 0
for _name, _n in (("ident", P), ("ubase", S), ("vbase", 2 * S), ("pix", H), ("loc", LOC), ("thr", CELLS - 1),
                  ("before", E * E), ("mhalf", 4)):
    CI[_name] = (_at, _at + _n)
    _at += _n
NCONST = _at


def build(nc, x, affine, taps, dw_bias, vectors, W1, b1, W2, b2, table, out):
    x_d = x.rearrange("b h w c -> (b h w) c").rearrange("(t p) c -> p t c", p=P)
    out_d = out.rearrange("b h w c -> (b h w) c").rearrange("(t p) c -> p t c", p=P)

    with ExitStack() as ctx:
        def sb(name, shape, dtype=F32):
            return ctx.enter_context(nc.sbuf_tensor(name, shape, dtype))

        def bank(name):
            return ctx.enter_context(nc.psum_tensor(name, [P, 512], F32))

        def sem(name):
            return ctx.enter_context(nc.semaphore(name))

        const = sb("const", [P, NCONST])
        x_tok = sb("x_tok", [P, TILES, C])
        aff = sb("aff", [C + 1, 2 * C + 3 * S + E])
        w_in_s = aff[:, 0:C]
        w_out_s = aff[:, C:2 * C]
        w_om = aff[:, 2 * C:2 * C + 3 * S]
        w_r = aff[:, 2 * C + 3 * S:]
        dw_diag = sb("dw_diag", [C + 1, K2, C])
        vec = sb("vec", [C, 2 + E + E * (C + 1)])
        gam = vec[:, 0:1]
        bet = vec[:, 1:2]
        lng_t = vec[:, 2:2 + E]
        lnb_col = vec[:, 2 + E:].rearrange("c (e m) -> c e m", e=E)
        w1_s = sb("w1_s", [C + 1, E * HID])
        w2_s = sb("w2_s", [P, E * HC, C])
        b2_bc = sb("b2_bc", [P, E * C])
        ident = const[:, CI["ident"][0]:CI["ident"][1]]
        before = const[:, CI["before"][0]:CI["before"][1]]
        mhalf = const[:, CI["mhalf"][0]:CI["mhalf"][1]]
        pix = const[:, CI["pix"][0]:CI["pix"][1]].unsqueeze(1)
        loc = const[:, CI["loc"][0]:CI["loc"][1]].unsqueeze(1)
        thr = const[:, CI["thr"][0]:CI["thr"][1]].unsqueeze(1)
        ubase = const[:, CI["ubase"][0]:CI["ubase"][1]].rearrange("p (q k g) -> p q k g", q=Q, g=2)
        vbase = [const[:, CI["vbase"][0] + h * S:CI["vbase"][0] + (h + 1) * S]
                 .rearrange("p (q k g) -> p q k g", q=Q, g=2) for h in range(2)]

        ln_sum = [sb(f"ln_sum{n}", [P, TP]) for n in range(4)]
        ln_mean = [sb(f"ln_mean{n}", [P, TP]) for n in range(4)]
        ln_ss = [sb(f"ln_ss{n}", [P, TP]) for n in range(4)]
        ln_var = [sb(f"ln_var{n}", [P, TP]) for n in range(4)]
        ln_rstd = [sb(f"ln_rstd{n}", [P, TP]) for n in range(4)]
        ln_xc = [sb(f"ln_xc{n}", [P, TP, C]) for n in range(4)]
        ln_sq = sb("ln_sq", [P, TP, C])

        x_in = sb("x_in", [P, TP, C])
        xn = sb("xn", [P, TP, C])
        xpad = sb("xpad", [C + 1, 3, 2, H + 2, W])
        x1n = sb("x1n", [P, TP, C])
        x1_t = sb("x1_t", [C + 1, TP * P])
        v_hi = sb("v_hi", [P, B, Q, GC, 2, LOC], F16)
        v_lo = sb("v_lo", [P, B, Q, GC, 2, LOC], F16)
        u = sb("u", [P, TP, S])
        v = sb("v", [P, TP, S])
        mx = sb("mx", [P, TP, G])
        es = sb("es", [P, TP, S])
        ex = es
        esum = sb("esum", [P, TP * Q, 2])
        rsum = sb("rsum", [P, TP * Q, 2])
        mask = es[:].rearrange("p t s -> p (t s)")
        past = sb("past", [P, TP * S, CELLS + 1])
        cell = sb("cell", [P, TP * S])
        uloc = cell
        dl = sb("dl", [P, TP * S, LOC])
        dv = [sb(f"dv{r}", [P, S, H]) for r in range(DR)]
        onehot = sb("onehot", [P, 2, TP * S, CELLS])
        hat_y = sb("hat_y", [P, 2, TP * S, H])
        hat_part = hat_y[:].rearrange("p o s y -> p o (s y)").bitcast(F16).rearrange("p o (n h) -> p o n h", h=2)
        wx = sb("wx", [P, 2, TP * NP, 2 * LOC])
        wk = [sb(f"wk{r}", [P, SC, H, CELLS]) for r in range(2)]
        wk_t = [sb(f"wk_t{r}", [P, TR, P]) for r in range(3)]
        prod = [sb(f"prod{r}", [P, NP, GC, 2 * LOC]) for r in range(2)]
        dw_bc = prod[0][0:C, :, :, :].rearrange("p n c l -> p (n c l)")[:, 0:K2 * C]
        w1_raw = prod[1][0:C, :, :, :].rearrange("p n c l -> p (n c l)")[:, 0:E * HID]
        samp = sb("samp", [P, TP, G, GC])
        samp_t = sb("samp_t", [C + 1, TP * P])
        x2 = sb("x2", [P, TP, C])
        out_s = x_tok
        z = sb("z", [P, TP, C])
        zn = sb("zn", [P, TP, C])
        z_t = samp_t
        zn_t = sb("zn_t", [C + 1, TP * P])
        lg = sb("lg", [P, TP, E])
        lmax = sb("lmax", [P, TP])
        le = sb("le", [P, TP, E])
        lx = sb("lx", [P, TP, E])
        cmp_gt = sb("cmp_gt", [P, TP, E, E])
        cmp_eq = sb("cmp_eq", [P, TP, E, E])
        rank = sb("rank", [P, TP, E])
        rank_eq = sb("rank_eq", [P, TP, E])
        top = sb("top", [P, TP, E])
        ptop = sb("ptop", [P, TP, E])
        psm = sb("psm", [P, TP])
        prs = sb("prs", [P, TP])
        wexp = sb("wexp", [P, TP, E])
        h_t = [sb(f"h_t{r}", [P, HC, 2 * P]) for r in range(HR)]
        y_sb = sb("y_sb", [P, E // 2, 2 * P])
        yb = sb("yb", [P, 2 * E, C])
        ysum = sb("ysum", [P, 2, C])

        tr_ps = [bank(f"tr_ps{r}") for r in range(2)]
        ga_ps = [bank(f"ga_ps{r}") for r in range(2)]
        m_ps = [bank(f"m_ps{r}") for r in range(4)]

        s_x = sem("s_x")
        s_tab = sem("s_tab")
        s_wa = sem("s_wa")
        s_wd = sem("s_wd")
        s_set = sem("s_set")
        s_zero = sem("s_zero")
        s_dwd = sem("s_dwd")
        s_lnb_ps = sem("s_lnb_ps")
        s_w1 = sem("s_w1")
        s_chain = sem("s_chain")
        s_var = [sem(f"s_var{n}") for n in range(4)]
        s_rstd = [sem(f"s_rstd{n}") for n in range(4)]
        s_xn = sem("s_xn")
        s_xnT = sem("s_xnT")
        s_xpad = sem("s_xpad")
        s_conv = sem("s_conv")
        s_vps = sem("s_vps")
        s_vblk = sem("s_vblk")
        s_conv_rd = sem("s_conv_rd")
        s_x1n = sem("s_x1n")
        s_x1nT = sem("s_x1nT")
        s_x1t = sem("s_x1t")
        s_om = sem("s_om")
        s_es = sem("s_es")
        s_ex = sem("s_ex")
        s_dl = sem("s_dl")
        s_dv = sem("s_dv")
        s_absl = sem("s_absl")
        s_absv = sem("s_absv")
        s_hx = sem("s_hx")
        s_haty = sem("s_haty")
        s_hat = sem("s_hat")
        s_hlo = sem("s_hlo")
        s_vlo = sem("s_vlo")
        s_win = sem("s_win")
        s_ysb = sem("s_ysb")
        s_yt = sem("s_yt")
        s_oneh = sem("s_oneh")
        s_wx = sem("s_wx")
        s_wk = sem("s_wk")
        s_tr = sem("s_tr")
        s_wkt = sem("s_wkt")
        s_ga = sem("s_ga")
        s_ga_rd = sem("s_ga_rd")
        s_samp = sem("s_samp")
        s_sT = sem("s_sT")
        s_st = sem("s_st")
        s_proj = sem("s_proj")
        s_x2 = sem("s_x2")
        s_z = sem("s_z")
        s_zn = sem("s_zn")
        s_zT = sem("s_zT")
        s_znT = sem("s_znT")
        s_zt = sem("s_zt")
        s_znt = sem("s_znt")
        s_lg = sem("s_lg")
        s_lg_rd = sem("s_lg_rd")
        s_le = sem("s_le")
        s_lx = sem("s_lx")
        s_h = sem("s_h")
        s_ht = sem("s_ht")
        s_y_mm = sem("s_y_mm")
        s_y_rd = sem("s_y_rd")
        s_out = sem("s_out")
        s_st_out = sem("s_st_out")

        N_X, N_TAB, N_WA, N_WD = 16, 16, 16 * 4, 16 * 4

        block = ctx.enter_context(nc.Block())

        @block.sync
        def _(sp):
            sp.dma_start(x_tok[:], x_d).then_inc(s_x, 16)
            sp.dma_start(const[:], table).then_inc(s_tab, 16)
            sp.dma_start(dw_bc, taps.to_broadcast([C, K2 * C])).then_inc(s_wa, 16)
            sp.dma_start(aff[:], affine).then_inc(s_wa, 16)
            sp.dma_start(vec[:], vectors).then_inc(s_wa, 16)
            sp.wait_ge(s_zero, 1)
            sp.dma_start(dw_diag[C:C + 1, K2 // 2, :], dw_bias).then_inc(s_wa, 16)
            sp.dma_start(w1_raw, W1).then_inc(s_wd, 16)
            sp.dma_start(w1_s[C:C + 1, :], b1).then_inc(s_wd, 16)
            sp.dma_start(w2_s[:].rearrange("p a c -> p (a c)"), W2).then_inc(s_wd, 16)
            sp.dma_start(b2_bc[:], b2.to_broadcast([P, E * C])).then_inc(s_wd, 16)
            with sp.Fori(0, B) as b:
                sp.wait_ge(s_out, b + 1)
                sp.dma_start(out_d[:, bass.ds(2 * b, 2), :], out_s[:, bass.ds(2 * b, 2), :]).then_inc(s_st_out, 16)
            sp.wait_ge(s_st_out, 16 * B)

        @block.gpsimd
        def _(pool):
            pool.memset(dw_diag[:], 0.0).then_inc(s_zero, 1)
            pool.memset(xpad[:], 0.0)
            pool.memset(v_hi[:], 0.0)
            pool.memset(v_lo[:], 0.0)
            pool.memset(past[:, :, 0:1], 1.0)
            pool.memset(past[:, :, CELLS:CELLS + 1], 0.0).then_inc(s_zero, 1)
            pool.wait_ge(s_zero, 2)
            pool.memset(xpad[C:C + 1, 1, :, 1:H + 1, :], 1.0)
            pool.memset(xpad[C:C + 1, 0, :, 1:H + 1, 1:W], 1.0)
            pool.memset(x1_t[C:C + 1, :], 1.0)
            pool.memset(samp_t[C:C + 1, :], 1.0)
            pool.memset(zn_t[C:C + 1, :], 1.0).then_inc(s_zero, 1)
            pool.wait_ge(s_tab, N_TAB)
            pool.wait_ge(s_zero, 3)

            def rstd(n, count):
                pool.wait_ge(s_var[n], count)
                pool.tensor_tensor(ln_rstd[n][:], ln_var[n][:], mhalf, ALU.pow).then_inc(s_rstd[n], 1)

            def hat_low(a, t):
                pool.wait_ge(s_haty, TP * a + t + 1)
                words = hat_part[:, bass.ds(a % 2, 1), t * (S * H):(t + 1) * (S * H), :]
                pool.tensor_tensor(words[:, :, :, 0].rearrange("p o n -> p (o n)"), dv[t % DR][:].rearrange("p s y -> p (s y)"),
                                   words[:, :, :, 1].rearrange("p o n -> p (o n)"), ALU.subtract).then_inc(s_hlo, 1)

            def body(j, has_a, has_d):
                for c in range(TP * WC):
                    if c == 0:
                        pool.wait_ge(s_hlo, TP * (j + 1))
                        pool.wait_ge(s_oneh, j + 1)
                    if c >= 2 or not first(j):
                        pool.wait_ge(s_tr, j * (TP * NG) + (c - 1) * (NG // WC))
                    pool.tensor_tensor(wk[c % 2][:],
                                       hat_y[:, bass.ds(j % 2, 1), c * SC:(c + 1) * SC, :].rearrange("p o s y -> p (o s) y")
                                       .unsqueeze(3).to_broadcast([P, SC, H, CELLS]),
                                       onehot[:, bass.ds(j % 2, 1), c * SC:(c + 1) * SC, :].rearrange("p o s y -> p (o s) y")
                                       .unsqueeze(2).to_broadcast([P, SC, H, CELLS]),
                                       ALU.mult).then_inc(s_wk, 1)
                    if c == 1 and has_a:
                        rstd(0, j + 2)
                    if c == 2 and has_d:
                        rstd(2, j)
                    if c == 3 and has_a:
                        rstd(1, j + 2)
                    if c == 3 and has_d:
                        rstd(3, j)
                    if has_a and c >= 8:
                        hat_low(j + 1, c - 8)

            rstd(0, 1)
            rstd(1, 1)
            for t in range(TP):
                hat_low(0, t)
            body(0, True, False)
            with pool.Fori(1, PAIRS - 1) as j:
                body(j, True, True)
            body(PAIRS - 1, False, True)
            rstd(2, PAIRS)
            rstd(3, PAIRS)

        @block.vector
        def _(dve):
            chain = [0, 0]

            def link(ins):
                chain[1] += 1
                ins.then_inc(s_chain, 1)
                dve.wait_ge(s_chain, chain[0] + chain[1])

            def moments(n, src, eps, read=None):
                link(dve.tensor_reduce(ln_sum[n][:], src, axis=AX.X, op=ALU.add))
                link(dve.tensor_scalar(ln_mean[n][:], ln_sum[n][:], 1.0 / C, None, ALU.mult))
                ins = dve.tensor_tensor(ln_xc[n][:], src, ln_mean[n][:].unsqueeze(2).to_broadcast([P, TP, C]), ALU.subtract)
                if read is None:
                    link(ins)
                else:
                    ins.then_inc(read[0], 1)
                    dve.wait_ge(read[0], read[1])
                link(dve.tensor_tensor(ln_sq[:], ln_xc[n][:], ln_xc[n][:], ALU.mult))
                link(dve.tensor_reduce(ln_ss[n][:], ln_sq[:], axis=AX.X, op=ALU.add))
                dve.tensor_scalar(ln_var[n][:], ln_ss[n][:], 1.0 / C, eps, ALU.mult, ALU.add).then_inc(s_var[n], 1)

            def normalise(n, dst, count, done):
                dve.wait_ge(s_rstd[n], count)
                dve.tensor_tensor(dst, ln_xc[n][:], ln_rstd[n][:].unsqueeze(2).to_broadcast([P, TP, C]),
                                  ALU.mult).then_inc(done, 1)

            def input_moments(a):
                link(dve.tensor_copy(x_in[:], x_tok[:, bass.ds(a * TP, TP), :]))
                moments(0, x_in[:], 1e-6)

            def conv_moments(a):
                dve.wait_ge(s_conv, a + 1)
                moments(1, m_ps[2][:, 0:TP * C].rearrange("p (t c) -> p t c", c=C), 1e-6, (s_conv_rd, a + 1))

            def om_tile(t):
                return m_ps[2 + t // 2][:, 256 * (t % 2):256 * (t % 2) + 3 * S]

            def image_low(a):
                dve.wait_ge(s_vblk, a + 1)
                for i in range(2):
                    for g in range(2):
                        src = m_ps[3 - 3 * i][g * KC:(g + 1) * KC, 0:LOC * C].rearrange("p (l q g c) -> p g q c l", l=LOC, q=Q, g=2)
                        lo, hi = (v[g * KC:(g + 1) * KC, bass.ds(2 * a + i, 1), :, :, g, :]
                                  .rearrange("p o q c l -> p (o q) c l") for v in (v_lo, v_hi))
                        ins = dve.tensor_tensor(lo, src[:, g, :, :, :], hi, ALU.subtract)
                ins.then_inc(s_vlo, 1)

            def coordinates(a):
                dve.wait_ge(s_om, a + 1)
                for t in range(TP):
                    off = om_tile(t)[:, 0:2 * S].rearrange("p (q g k o) -> p q k g o", q=Q, g=2, k=K2)
                    dve.tensor_tensor(u[:, t, :].rearrange("p (q k g) -> p q k g", q=Q, g=2), off[:, :, :, :, 0],
                                      ubase, ALU.add)
                    dve.tensor_tensor(v[:, t, :].rearrange("p (q k g) -> p q k g", q=Q, g=2), off[:, :, :, :, 1],
                                      vbase[t % 2], ALU.add)
                    ins = dve.tensor_reduce(mx[:, t, :], om_tile(t)[:, 2 * S:3 * S].rearrange("p (g k) -> p g k", k=K2),
                                            axis=AX.X, op=ALU.max)
                link(ins)
                for t in range(TP):
                    ins = dve.tensor_tensor(es[:, t, :].rearrange("p (q k g) -> p q k g", q=Q, g=2),
                                            om_tile(t)[:, 2 * S:3 * S].rearrange("p (q g k) -> p q k g", q=Q, g=2),
                                            mx[:, t, :].rearrange("p (q g) -> p q g", g=2).unsqueeze(2)
                                            .to_broadcast([P, Q, K2, 2]), ALU.subtract)
                ins.then_inc(s_es, 1)

            def cells(a):
                uf = u[:].rearrange("p t s -> p (t s)").unsqueeze(2)
                link(dve.tensor_tensor(past[:, :, 1:CELLS], uf.to_broadcast([P, TP * S, CELLS - 1]),
                                       thr.to_broadcast([P, TP * S, CELLS - 1]), ALU.is_ge))
                if not first(a):
                    dve.wait_ge(s_wk, (a - 1) * (TP * WC))
                dve.tensor_tensor(onehot[:, bass.ds(a % 2, 1), :, :].rearrange("p o s c -> p (o s) c"), past[:, :, 0:CELLS],
                                  past[:, :, 1:CELLS + 1], ALU.subtract).then_inc(s_oneh, 1)
                link(dve.tensor_reduce(cell[:], past[:, :, 1:CELLS], axis=AX.X, op=ALU.add))
                link(dve.scalar_tensor_tensor(uloc[:], cell[:], -4.0, u[:].rearrange("p t s -> p (t s)"),
                                              ALU.mult, ALU.add))
                dve.tensor_tensor(dl[:], uloc[:].unsqueeze(2).to_broadcast([P, TP * S, LOC]),
                                  loc.to_broadcast([P, TP * S, LOC]), ALU.subtract).then_inc(s_dl, 1)

            def row_distance(a, t):
                if t >= DR or not first(a):
                    dve.wait_ge(s_hlo, TP * a + (t - DR if t >= DR else 0) + (1 if t >= DR else 0))
                dve.tensor_tensor(dv[t % DR][:], v[:, t, :].unsqueeze(2).to_broadcast([P, S, H]),
                                  pix.to_broadcast([P, S, H]), ALU.subtract).then_inc(s_dv, 1)

            def tap_weights(a):
                dve.wait_ge(s_ex, a + 1)
                exv = ex[:].rearrange("p t (q k g) -> p (t q) k g", q=Q, g=2)
                link(dve.tensor_reduce(esum[:], exv.rearrange("p q k g -> p q g k"), axis=AX.X, op=ALU.add))
                link(dve.reciprocal(rsum[:], esum[:]))
                link(dve.tensor_tensor(mask.rearrange("p (q k g) -> p q k g", k=K2, g=2), exv,
                                       rsum[:].unsqueeze(2).to_broadcast([P, TP * Q, K2, 2]), ALU.mult))
                dve.wait_ge(s_hx, a + 1)
                dve.tensor_tensor(wx[:, bass.ds(a % 2, 1), :, :].rearrange("p o n (g l) -> p (o n g) l", l=LOC),
                                  dl[:], mask.unsqueeze(2).to_broadcast([P, TP * S, LOC]),
                                  ALU.mult).then_inc(s_wx, 1)

            def weigh(j, t, n):
                dve.wait_ge(s_ga, j * (TP * NG) + t * NG + -(-(n + 1) * PB // TR))
                dve.tensor_tensor(
                    prod[t % 2][:, n * PB:(n + 1) * PB, :, :],
                    ga_ps[n % 2][:, 0:PB * NV].rearrange("p (n c l) -> p n c l", n=PB, c=GC),
                    wx[:, bass.ds(j % 2, 1), t * NP + n * PB:t * NP + (n + 1) * PB, :].rearrange("p o n l -> p (o n) l")
                    .unsqueeze(2).to_broadcast([P, PB, GC, 2 * LOC]), ALU.mult).then_inc(s_ga_rd, 1)

            def tile_sum(j, t):
                dve.wait_ge(s_ga_rd, j * (TP * NBK) + (t + 1) * NBK)
                if t == 0 and not first(j):
                    dve.wait_ge(s_sT, j)
                for q in range(Q):
                    ins = dve.tensor_reduce(
                        samp[:, t, 2 * q:2 * q + 2, :],
                        prod[t % 2][:, q * K2:(q + 1) * K2, :, :].rearrange("p k c (g l) -> p g c k l", g=2),
                        axis=AX.XY, op=ALU.add)
                if t == TP - 1:
                    ins.then_inc(s_samp, 1)

            def residual(d, weighed=None):
                dve.wait_ge(s_proj, d + 1)
                if last(d):
                    dve.wait_ge(s_out, 2 * d)
                else:
                    dve.wait_ge(s_ga_rd, weighed)
                dve.tensor_tensor(x2[:], m_ps[1][:, 0:TP * C].rearrange("p (t c) -> p t c", c=C),
                                  x_tok[:, bass.ds(d * TP, TP), :], ALU.add).then_inc(s_x2, 1)
                dve.wait_ge(s_x2, d + 1)
                moments(2, x2[:], 1e-5)

            def inner_norm(d):
                normalise(2, z[:], d + 1, s_z)
                dve.wait_ge(s_z, d + 1)
                moments(3, z[:], 1e-5)

            def route(d):
                dve.wait_ge(s_lg, d + 1)
                dve.tensor_copy(lg[:], m_ps[1][:, 0:TP * E].rearrange("p (t e) -> p t e", e=E)).then_inc(s_lg_rd, 1)
                dve.wait_ge(s_lg_rd, d + 1)
                link(dve.tensor_reduce(lmax[:], lg[:], axis=AX.X, op=ALU.max))
                dve.tensor_tensor(le[:], lg[:], lmax[:].unsqueeze(2).to_broadcast([P, TP, E]),
                                  ALU.subtract).then_inc(s_le, 1)
                for t in range(TP):
                    other = lg[:, t, :].unsqueeze(1).to_broadcast([P, E, E])
                    own = lg[:, t, :].unsqueeze(2).to_broadcast([P, E, E])
                    dve.tensor_tensor(cmp_gt[:, t, :, :], other, own, ALU.is_gt)
                    ins = dve.tensor_tensor(cmp_eq[:, t, :, :], other, own, ALU.is_equal)
                link(ins)
                link(dve.tensor_tensor(cmp_eq[:].rearrange("p t i j -> p t (i j)"), cmp_eq[:].rearrange("p t i j -> p t (i j)"),
                                       before.unsqueeze(1).to_broadcast([P, TP, E * E]), ALU.mult))
                dve.tensor_reduce(rank[:], cmp_gt[:], axis=AX.X, op=ALU.add)
                link(dve.tensor_reduce(rank_eq[:], cmp_eq[:], axis=AX.X, op=ALU.add))
                link(dve.tensor_tensor(rank[:], rank[:], rank_eq[:], ALU.add))
                link(dve.tensor_scalar(top[:], rank[:], 2.0, None, ALU.is_lt))

            def expert_weights(d):
                dve.wait_ge(s_lx, d + 1)
                link(dve.tensor_tensor(ptop[:], lx[:], top[:], ALU.mult))
                link(dve.tensor_reduce(psm[:], ptop[:], axis=AX.X, op=ALU.add))
                link(dve.reciprocal(prs[:], psm[:]))
                link(dve.tensor_tensor(wexp[:], ptop[:], prs[:].unsqueeze(2).to_broadcast([P, TP, E]), ALU.mult))

            def combine(d, i):
                dve.wait_ge(s_yt, 2 * d + i + 1)
                for t in range(2):
                    ins = dve.tensor_tensor(yb[:, t * E:(t + 1) * E, :],
                                            m_ps[2 + t][:, :].rearrange("p (e c) -> p e c", c=C),
                                            b2_bc[:].rearrange("p (e c) -> p e c", c=C), ALU.add)
                ins.then_inc(s_y_rd, 1)
                dve.wait_ge(s_y_rd, 2 * d + i + 1)
                wv = wexp[:, 2 * i:2 * i + 2, :].rearrange("p t e -> p (t e)").unsqueeze(2)
                link(dve.tensor_tensor(yb[:], yb[:],
                                       wv.to_broadcast([P, 2 * E, C]), ALU.mult))
                link(dve.tensor_reduce(ysum[:], yb[:].rearrange("p (t e) c -> p t c e", e=E), axis=AX.X, op=ALU.add))
                dve.tensor_tensor(out_s[:, bass.ds(d * TP + 2 * i, 2), :], ysum[:], x2[:, 2 * i:2 * i + 2, :], ALU.add).then_inc(s_out, 1)

            def body(j, has_a, has_d):
                dve.wait_ge(s_wx, j + 1)
                for m in range(TP * NBK):
                    if has_a:
                        if m == 0:
                            input_moments(j + 1)
                        if m == 2:
                            normalise(0, xn[:], j + 2, s_xn)
                        if m == 5:
                            conv_moments(j + 1)
                        if m == 7:
                            image_low(j + 1)
                        if m == 8:
                            normalise(1, x1n[:], j + 2, s_x1n)
                        if m == 12:
                            coordinates(j + 1)
                        if m == 13:
                            cells(j + 1)
                        if m in (14, 15, 16, 17):
                            row_distance(j + 1, m - 14)
                        if m == 18:
                            tap_weights(j + 1)
                    if has_d:
                        if m == 3:
                            residual(j - 1, j * (TP * NBK) + 3)
                        if m == 5:
                            inner_norm(j - 1)
                        if m == 7:
                            normalise(3, zn[:], j, s_zn)
                        if m == 9:
                            route(j - 1)
                        if m == 11:
                            expert_weights(j - 1)
                        if m == 19:
                            combine(j - 1, 0)
                    weigh(j, m // NBK, m % NBK)
                    if m % NBK == NBK - 1:
                        tile_sum(j, m // NBK)
                if has_d:
                    combine(j - 1, 1)

            dve.wait_ge(s_x, N_X)
            input_moments(0)
            dve.wait_ge(s_tab, N_TAB)
            dve.wait_ge(s_wa, N_WA)
            dve.tensor_tensor(dw_diag[0:C, :, :], ident[0:C, 0:C].unsqueeze(1).to_broadcast([C, K2, C]),
                              dw_bc.rearrange("p (k c) -> p k c", c=C), ALU.mult).then_inc(s_dwd, 1)
            dve.tensor_scalar(w_in_s, w_in_s, V_SCALE, None, ALU.mult).then_inc(s_win, 1)
            dve.wait_ge(s_zero, 3)
            normalise(0, xn[:], 1, s_xn)
            conv_moments(0)
            image_low(0)
            normalise(1, x1n[:], 1, s_x1n)
            coordinates(0)
            cells(0)
            row_distance(0, 0)
            row_distance(0, 1)
            tap_weights(0)
            row_distance(0, 2)
            row_distance(0, 3)
            dve.wait_ge(s_wd, N_WD)
            for e in range(E):
                dve.tensor_scalar(w1_s[0:C, e * HID:(e + 1) * HID], w1_raw[:, e * HID:(e + 1) * HID],
                                  lng_t[:, e:e + 1], None, ALU.mult)
            dve.wait_ge(s_lnb_ps, 1)
            for n in range(4):
                ins = dve.tensor_tensor(w1_s[C:C + 1, n * 512:(n + 1) * 512], m_ps[n][C:C + 1, :],
                                        w1_s[C:C + 1, n * 512:(n + 1) * 512], ALU.add)
            ins.then_inc(s_w1, 1)

            body(0, True, False)
            before_loop, chain[1] = chain[1], 0
            with dve.Fori(1, PAIRS - 1) as j:
                chain[0] = (j - 1) * LINKS + before_loop
                body(j, True, True)
            assert chain[1] == LINKS, chain[1]
            chain[0], chain[1] = before_loop + (PAIRS - 2) * LINKS, 0
            body(PAIRS - 1, False, True)
            residual(PAIRS - 1)
            inner_norm(PAIRS - 1)
            normalise(3, zn[:], PAIRS, s_zn)
            route(PAIRS - 1)
            expert_weights(PAIRS - 1)
            combine(PAIRS - 1, 0)
            combine(PAIRS - 1, 1)

        @block.scalar
        def _(act):
            act.wait_ge(s_zero, 3)
            act.wait_ge(s_wa, N_WA)

            def pad_image(a):
                act.wait_ge(s_xnT, a + 1)
                if not first(a):
                    act.wait_ge(s_vps, a)
                src = m_ps[0][0:C, :].rearrange("c (i y x) -> c i y x", i=2, y=H)
                for dx in range(3):
                    lo, hi = max(0, 1 - dx), min(W, W + 1 - dx)
                    ins = act.copy(xpad[0:C, dx, :, 1:H + 1, lo:hi], src[:, :, :, lo + dx - 1:hi + dx - 1])
                ins.then_inc(s_xpad, 1)

            def block_diagonal(a):
                act.wait_ge(s_vps, a + 1)
                for i in range(2):
                    for g in range(2):
                        src = m_ps[3 - 3 * i][g * KC:(g + 1) * KC, 0:LOC * C].rearrange("p (l q g c) -> p g q c l", l=LOC, q=Q, g=2)
                        ins = act.copy(v_hi[g * KC:(g + 1) * KC, bass.ds(2 * a + i, 1), :, :, g, :]
                                       .rearrange("p o q c l -> p (o q) c l"), src[:, g, :, :, :])
                ins.then_inc(s_vblk, 1)

            def conv_gelu(a):
                act.wait_ge(s_x1nT, a + 1)
                act.activation(x1_t[0:C, :], m_ps[0][0:C, :], ACT.Gelu, bias=bet, scale=gam).then_inc(s_x1t, 1)

            def tap_exp(a):
                act.wait_ge(s_es, a + 1)
                act.activation(ex[:], es[:], ACT.Exp).then_inc(s_ex, 1)

            def hat_x(a):
                act.wait_ge(s_dl, a + 1)
                act.activation(dl[:], dl[:], ACT.Abs).then_inc(s_absl, 1)
                act.wait_ge(s_absl, a + 1)
                act.activation(dl[:], dl[:], ACT.Relu, bias=1.0 / (W_SCALE * V_SCALE), scale=-1.0 / (W_SCALE * V_SCALE)).then_inc(s_hx, 1)

            def hat_rows(a, t):
                act.wait_ge(s_dv, a * TP + t + 1)
                act.activation(dv[t % DR][:], dv[t % DR][:], ACT.Abs).then_inc(s_absv, 1)
                act.wait_ge(s_absv, a * TP + t + 1)
                if t == 0 and not first(a):
                    act.wait_ge(s_wk, (a - 1) * (TP * WC))
                act.activation(dv[t % DR][:], dv[t % DR][:], ACT.Relu, bias=W_SCALE, scale=-W_SCALE).then_inc(s_hat, 1)
                act.wait_ge(s_hat, a * TP + t + 1)
                act.copy(hat_part[:, bass.ds(a % 2, 1), t * (S * H):(t + 1) * (S * H), 1].rearrange("p o n -> p (o n)"),
                         dv[t % DR][:].rearrange("p s y -> p (s y)")).then_inc(s_haty, 1)

            def samples_out(d):
                act.wait_ge(s_sT, d + 1)
                act.copy(samp_t[0:C, :], m_ps[1][0:C, :]).then_inc(s_st, 1)

            def z_out(d):
                act.wait_ge(s_zT, d + 1)
                act.copy(z_t[0:C, :], m_ps[1][0:C, :]).then_inc(s_zt, 1)

            def zn_out(d):
                act.wait_ge(s_znT, d + 1)
                act.copy(zn_t[0:C, :], m_ps[0][0:C, :]).then_inc(s_znt, 1)

            def router_exp(d):
                act.wait_ge(s_le, d + 1)
                act.activation(lx[:], le[:], ACT.Exp).then_inc(s_lx, 1)

            def hidden(d, n):
                act.wait_ge(s_h, d * (2 * E) + n + 1)
                if n >= HR or last(d):
                    act.wait_ge(s_y_mm, d * (2 * E) + n - HR + 1)
                act.activation(h_t[n % HR][:].rearrange("p a n -> p (a n)"), m_ps[n % 2][:, :], ACT.Gelu).then_inc(s_ht, 1)

            def outputs_out(d, i):
                act.wait_ge(s_y_mm, d * (2 * E) + (i + 1) * E)
                if i == 1 or last(d):
                    act.wait_ge(s_yt, 2 * d + i)
                for b in range(2):
                    ins = act.copy(y_sb[:, 2 * b:2 * b + 2, :].rearrange("p e n -> p (e n)"), m_ps[2 + b][:, :])
                ins.then_inc(s_ysb, 1)

            def body(j, has_a, has_d):
                for n in range(TP * NG):
                    act.wait_ge(s_tr, j * (TP * NG) + n + 1)
                    if n >= 3 or not first(j):
                        act.wait_ge(s_ga, j * (TP * NG) + n - 2)
                    act.copy(wk_t[n % 3][:], tr_ps[n % 2][:, :].rearrange("p (n m) -> p n m", n=TR)).then_inc(s_wkt, 1)
                    if has_d:
                        if n == 2:
                            samples_out(j - 1)
                        if n == 10:
                            z_out(j - 1)
                        if n == 16:
                            router_exp(j - 1)
                        if n == 13:
                            zn_out(j - 1)
                    if has_a:
                        if n == 5:
                            pad_image(j + 1)
                        if n == 8:
                            block_diagonal(j + 1)
                        if n == 15:
                            conv_gelu(j + 1)
                        if n == 20:
                            tap_exp(j + 1)
                        if n == 21:
                            hat_x(j + 1)
                        if n in (23, 25, 26, 28):
                            hat_rows(j + 1, (23, 25, 26, 28).index(n))
                    if has_d:
                        for unit in range(2 * E):
                            if n == ACT_UNIT[unit]:
                                hidden(j - 1, unit)
                        if n == 27:
                            outputs_out(j - 1, 0)
                if has_d:
                    outputs_out(j - 1, 1)

            pad_image(0)
            block_diagonal(0)
            conv_gelu(0)
            tap_exp(0)
            hat_x(0)
            for t in range(TP):
                hat_rows(0, t)
            body(0, True, False)
            with act.Fori(1, PAIRS - 1) as j:
                body(j, True, True)
            body(PAIRS - 1, False, True)
            samples_out(PAIRS - 1)
            z_out(PAIRS - 1)
            router_exp(PAIRS - 1)
            zn_out(PAIRS - 1)
            for n in range(2 * E):
                if n == E:
                    outputs_out(PAIRS - 1, 0)
                hidden(PAIRS - 1, n)
            outputs_out(PAIRS - 1, 1)

        @block.tensor
        def _(pe):
            pe.wait_ge(s_tab, N_TAB)
            pe.wait_ge(s_wa, N_WA)
            pe.wait_ge(s_zero, 3)
            pe.wait_ge(s_dwd, 1)
            pe.wait_ge(s_win, 1)

            def transposes(src, dst):
                for t in range(TP):
                    if t == 0:
                        ins = pe.transpose(dst[:, 0:P], src[:, 0:2, :].rearrange("p t c -> p (t c)"), ident)
                    else:
                        ins = pe.transpose(dst[0:C, t * P:(t + 1) * P], src[:, t, :], ident)
                return ins

            def input_t(a):
                pe.wait_ge(s_xn, a + 1)
                transposes(xn, m_ps[0]).then_inc(s_xnT, 1)

            def convolve(a):
                pe.wait_ge(s_xpad, a + 1)
                for t in range(TP):
                    y0 = (t % 2) * (H // 2)
                    for k in range(K2):
                        dy, dx = k // 3, k % 3
                        ins = pe.matmul(m_ps[2][:, t * C:(t + 1) * C],
                                        xpad[:, dx, t // 2, y0 + dy:y0 + dy + H // 2, :].rearrange("c y x -> c (y x)"),
                                        dw_diag[:, k, :], start=(k == 0), stop=(k == K2 - 1))
                ins.then_inc(s_conv, 1)

            def project_in(a):
                for i in range(2):
                    for l in range(LOC):
                        px = xpad[:, min(l, 1), i, 1:H + 1, :].rearrange("c y x -> c (y x)")[:, max(l - 1, 0)::CELLS]
                        for g in range(2):
                            ins = pe.matmul(m_ps[3 - 3 * i][g * KC:(g + 1) * KC, l * C:(l + 1) * C], px, w_in_s,
                                            start=True, stop=True)
                ins.then_inc(s_vps, 1)

            def conv_t(a, d=None):
                if d is not None:
                    pe.wait_ge(s_znt, d + 1)
                pe.wait_ge(s_x1n, a + 1)
                pe.wait_ge(s_vlo, a + 1)
                transposes(x1n, m_ps[0]).then_inc(s_x1nT, 1)

            def offsets(a):
                pe.wait_ge(s_x1t, a + 1)
                for t in range(TP):
                    ins = pe.matmul(m_ps[2 + t // 2][:, 256 * (t % 2):256 * (t % 2) + 3 * S],
                                    x1_t[:, t * P:(t + 1) * P], w_om, start=True, stop=True)
                ins.then_inc(s_om, 1)

            def transpose_weights(j, n):
                e = n % NG
                per = NG // WC
                c = (n // NG) * WC + e // per
                if e % per == 0:
                    pe.wait_ge(s_wk, j * (TP * WC) + c + 1)
                if n >= 2 or not first(j):
                    pe.wait_ge(s_wkt, j * (TP * NG) + n - 1)
                src = wk[c % 2][:].rearrange("p (n g) y x -> p n (g y x)", g=2)
                for i in range(TR):
                    ins = pe.transpose(tr_ps[n % 2][:, i * P:(i + 1) * P], src[:, (e % per) * TR + i, :], ident)
                ins.then_inc(s_tr, 1)

            def gather(j, n):
                pe.wait_ge(s_wkt, j * (TP * NG) + n + 1)
                t, e = n // NG, n % NG
                for i in range(TR):
                    p = e * TR + i
                    bk = t * NBK + p // PB
                    if p % PB == 0 and (bk >= 2 or not first(j)):
                        pe.wait_ge(s_ga_rd, j * (TP * NBK) + bk - 1)
                    v_h, v_l = (v[:, bass.ds(2 * j + t // 2, 1), p // K2, :, :, :].rearrange("p b c g l -> p (b c g l)")
                                for v in (v_hi, v_lo))
                    w_l, w_h = (wk_t[n % 3][:, i, :].bitcast(F16)[:, h::2] for h in range(2))
                    for w, v, st, sp in ((w_h, v_h, True, False), (w_h, v_l, False, False), (w_l, v_h, False, True)):
                        ins = pe.matmul(ga_ps[bk % 2][:, (p % PB) * NV:(p % PB + 1) * NV], w, v, start=st, stop=sp)
                ins.then_inc(s_ga, 1)

            def samples_t(d):
                pe.wait_ge(s_samp, d + 1)
                transposes(samp[:].rearrange("p t g c -> p t (g c)"), m_ps[1]).then_inc(s_sT, 1)

            def project_out(d):
                pe.wait_ge(s_st, d + 1)
                for t in range(TP):
                    ins = pe.matmul(m_ps[1][:, t * C:(t + 1) * C], samp_t[:, t * P:(t + 1) * P], w_out_s,
                                    start=True, stop=True)
                ins.then_inc(s_proj, 1)

            def router_t(d):
                pe.wait_ge(s_z, d + 1)
                transposes(z, m_ps[1]).then_inc(s_zT, 1)

            def router(d):
                pe.wait_ge(s_zt, d + 1)
                for t in range(TP):
                    ins = pe.matmul(m_ps[1][:, t * E:(t + 1) * E], z_t[:, t * P:(t + 1) * P], w_r, start=True, stop=True)
                ins.then_inc(s_lg, 1)

            def experts_t(d, images):
                pe.wait_ge(s_vlo, images)
                pe.wait_ge(s_zn, d + 1)
                transposes(zn, m_ps[0]).then_inc(s_znT, 1)

            def expert_in(d, n):
                if n == 0:
                    pe.wait_ge(s_znt, d + 1)
                if n == 1:
                    pe.wait_ge(s_lg_rd, d + 1)
                if n >= 2:
                    pe.wait_ge(s_ht, d * (2 * E) + n - 1)
                i, e = n // E, n % E
                for a in range(HC):
                    c0 = e * HID + a * P
                    ins = pe.matmul(m_ps[n % 2][:, a * 2 * P:(a + 1) * 2 * P], w1_s[:, c0:c0 + P],
                                    zn_t[:, i * 2 * P:(i + 1) * 2 * P], start=True, stop=True)
                ins.then_inc(s_h, 1)

            def expert_out(d, n, last_es):
                i, e = n // E, n % E
                pe.wait_ge(s_ht, d * (2 * E) + n + 1)
                if n == 0:
                    pe.wait_ge(s_es, last_es)
                if n == E:
                    pe.wait_ge(s_y_rd, 2 * d + 1)
                rows, c0 = (e % 2) * C, (e // 2 % 2) * 2 * P
                for a in range(HC):
                    ins = pe.matmul(m_ps[2 + e // 4][rows:rows + C, c0:c0 + 2 * P], w2_s[:, e * HC + a, :],
                                    h_t[n % HR][:, a, :], start=(a == 0), stop=(a == HC - 1))
                ins.then_inc(s_y_mm, 1)

            def outputs_t(d, i):
                pe.wait_ge(s_ysb, 2 * d + i + 1)
                for t in range(2):
                    for e in range(E // 2):
                        ins = pe.transpose(m_ps[2 + t][:, e * P:(e + 1) * P], y_sb[:, e, t * P:(t + 1) * P], ident)
                ins.then_inc(s_yt, 1)

            def body(j, has_a, has_d):
                for n in range(TP * NG):
                    transpose_weights(j, n)
                    if n > 0:
                        gather(j, n - 1)
                    elif not first(j):
                        gather(j - 1, TP * NG - 1)
                    if has_d:
                        if n == 1:
                            samples_t(j - 1)
                        if n == 3:
                            project_out(j - 1)
                        if n == 9:
                            router_t(j - 1)
                        if n == 11:
                            router(j - 1)
                        if n == 12:
                            experts_t(j - 1, j + 2 if has_a else PAIRS)
                    if has_a:
                        if n == 4:
                            input_t(j + 1)
                        if n == 6:
                            convolve(j + 1)
                        if n == 7:
                            project_in(j + 1)
                        if n == 14:
                            conv_t(j + 1, j - 1 if has_d else None)
                        if n == 16:
                            offsets(j + 1)
                    if has_d:
                        for unit in range(2 * E):
                            if n == PE_IN[unit]:
                                expert_in(j - 1, unit)
                            if n == PE_OUT[unit]:
                                expert_out(j - 1, unit, j + 2 if has_a else PAIRS)
                        if n == 28:
                            outputs_t(j - 1, 0)
                if has_d:
                    outputs_t(j - 1, 1)

            input_t(0)
            convolve(0)
            project_in(0)
            conv_t(0)
            offsets(0)
            pe.wait_ge(s_wd, N_WD)
            pe.wait_ge(s_es, 1)
            for e in range(E):
                ins = pe.matmul(m_ps[e // 2][0:C + 1, (e % 2) * HID:(e % 2 + 1) * HID], lnb_col[:, e, :],
                                w1_raw[:, e * HID:(e + 1) * HID], start=True, stop=True)
            ins.then_inc(s_lnb_ps, 1)
            pe.wait_ge(s_w1, 1)

            body(0, True, False)
            with pe.Fori(1, PAIRS - 1) as j:
                body(j, True, True)
            body(PAIRS - 1, False, True)
            gather(PAIRS - 1, TP * NG - 1)
            samples_t(PAIRS - 1)
            project_out(PAIRS - 1)
            router_t(PAIRS - 1)
            router(PAIRS - 1)
            experts_t(PAIRS - 1, PAIRS)
            for i in range(2):
                for n in range(E + 2):
                    if n < E:
                        expert_in(PAIRS - 1, i * E + n)
                    if n >= 2:
                        expert_out(PAIRS - 1, i * E + n - 2, PAIRS)
                outputs_t(PAIRS - 1, i)


def layout(inputs):
    import numpy as np
    f = lambda n: np.ascontiguousarray(inputs[n])
    c = lambda n: f("L0_conv_" + n)
    m = lambda n: f("L0_ffn_" + n)
    with_bias = lambda w, b: np.concatenate([w, b[None, :]], 0)
    lnb = np.zeros((C, E, C + 1), np.float32)
    lnb[:, :, C] = m("ln_b").T
    return {
        "x": f("x"),
        "affine": np.concatenate([with_bias(c("w_in"), c("b_in")), with_bias(c("w_out"), c("b_out")),
                                  with_bias(c("w_off"), c("b_off")), with_bias(c("w_mask"), c("b_mask")),
                                  with_bias(m("Wr"), m("br"))], 1),
        "taps": c("dw_kernel").reshape(1, K2 * C),
        "dw_bias": c("dw_bias").reshape(1, C),
        "vectors": np.concatenate([c("ln_gamma")[:, None], c("ln_beta")[:, None], m("ln_g").T, lnb.reshape(C, -1)], 1),
        "W1": m("W1").transpose(1, 0, 2).reshape(C, E * HID),
        "b1": m("b1").reshape(1, E * HID),
        "W2": m("W2").reshape(E * HC, P, C).transpose(1, 0, 2).reshape(P, E * HC * C),
        "b2": m("b2").reshape(1, E * C),
        "table": shape_table(),
    }


def shape_table():
    import numpy as np
    tab = np.zeros((P, NCONST), np.float32)
    put = lambda name, a: tab.__setitem__((slice(None), slice(*CI[name])), a)
    p = np.arange(P)[:, None]
    k = np.arange(K2)
    tap = lambda a: np.broadcast_to(a[:, None, :, None], (P, Q, K2, 2)).reshape(P, S)
    put("ident", np.eye(P))
    put("ubase", tap(p % W + k % 3 - 1))
    put("vbase", np.concatenate([tap(h * (H // 2) + p // W + k // 3 - 1) for h in range(2)], 1))
    put("pix", np.arange(H))
    put("loc", np.arange(LOC) - 1)
    put("thr", 4 * np.arange(1, CELLS) - 1)
    put("before", (np.arange(E)[None, :] < np.arange(E)[:, None]).reshape(1, -1))
    put("mhalf", -0.5)
    return tab


def kernel(**inputs):
    import numpy as _np
    import concourse.bacc as _bacc
    from concourse import mybir as _mybir
    from concourse.bass_utils import run_bass_kernel_spmd as _run

    nc = _bacc.Bacc("TRN2", target_bir_lowering=False, num_devices=1)
    arrays, args = {}, []
    for name, a in layout(inputs).items():
        a = _np.ascontiguousarray(a)
        arrays[f"in_{name}"] = a
        args.append(nc.dram_tensor(f"in_{name}", a.shape, _mybir.dt.from_np(a.dtype), kind="ExternalInput").ap())
    args.append(nc.dram_tensor("out_dram", (B, H, W, C), F32, kind="ExternalOutput").ap())
    build(nc, *args)
    r = _run(nc, [arrays], core_ids=[0])
    return r.results[0]["out_dram"]
```

```python
from contextlib import ExitStack

import concourse.bass as bass
from concourse import mybir

F32 = mybir.dt.float32
F16 = mybir.dt.float16
ALU = mybir.AluOpType
ACT = mybir.ActivationFunctionType
AX = mybir.AxisListType

P = 128
B, H, W, C = 8, 16, 16, 64
G, K2 = 8, 9
GC = C // G
Q = G // 2
S = G * K2
TILES = B * H * W // P
PAIRS = B // 2
TP = TILES // PAIRS
HW = H * W
CELLS, LOC = 4, 5
KC = H * CELLS
NV = GC * 2 * LOC
NP = Q * K2
TR = 4
NG = NP // TR
PB = 6
NBK = NP // PB
WC = 3
SC = S // WC
E, HID = 8, 256
HC = HID // P
HR = 4
DR = 3
AHEAD = 2
W_SCALE = 2.0 ** 8
V_SCALE = 2.0 ** 6
Z_SCALE = 2.0 ** 8
W1_SCALE = 2.0 ** 6
TAP_SCALE = 2.0 ** 6
LINKS = 41
BR = 33
NR = 97

PE_AT = {"samples_t": 2, "project_out": 3, "router_t": 9, "router": 11, "experts_t": 12, "outputs_t": [27, 35],
         "input_t": 5, "convolve": 8, "project_in": 8, "conv_t": 14, "offsets": 16,
         "expert_in": [18, 19, 21, 21, 22, 22, 23, 24, 25, 26, 27, 28, 29, 30, 31, 32],
         "expert_out": [21, 21, 22, 23, 23, 24, 25, 26, 29, 30, 30, 31, 31, 32, 33, 34], "bias_1": [3, 5, 7, 9]}
ACT_AT = {"samples_out": 2, "z_out": 10, "router_exp": 19, "zn_out": 13, "outputs_out": [26, 34], "pad_image": 5,
          "block_diagonal": 9, "conv_gelu": 15, "tap_exp": 19, "hat_x_abs": 22, "hat_x": 23,
          "hidden": [20, 20, 21, 22, 22, 23, 24, 25, 26, 27, 28, 29, 30, 31, 32, 33], "row_abs": [24, 29, 10, 15],
          "row_hat": [25, 30, 11, 16], "row_high": [26, 32, 12, 18], "w1_high": [20, 25, 30]}
DVE_AT = {"input_moments": 0, "input_norm": 2, "input_low": 4, "conv_moments": 5, "image_low": 7, "conv_norm": 8,
          "coordinates": 11, "row_distance": [15, 18, 6, 8], "tap_weights": 18, "residual": 4, "inner_norm": 5,
          "zn_norm": 7, "zn_low": 9, "route": 10, "expert_weights": 14, "bias_1": [2, 3, 4, 6], "w1_scale": 6,
          "w1_low": 21, "one_hots": 13, "distances": 13, "outputs_in": [18, 23], "combine": [19, 23]}
POOL_AT = {"rstd0": 2, "rstd1": 5, "rstd2": 2, "rstd3": 3, "hat_low": [9, 11, 5, 7]}
TAP_SUM_AT = [1, 3, 4, 5]


def first(i):
    return isinstance(i, int) and i == 0


def last(i):
    return isinstance(i, int) and i == PAIRS - 1


CI = {}
_at = 0
for _name, _n in (("ident", P), ("ubase", S), ("vbase", 2 * S), ("pix", H), ("loc", LOC), ("thr", CELLS - 1),
                  ("before", E * E), ("mhalf", 4)):
    CI[_name] = (_at, _at + _n)
    _at += _n
NCONST = _at


def build(nc, x, affine, taps, biases, vectors, W1, b1, W2, b2, table, out):
    x_d = x.rearrange("b h w c -> (b h w) c").rearrange("(t p) c -> p t c", p=P)
    out_d = out.rearrange("b h w c -> (b h w) c").rearrange("(t p) c -> p t c", p=P)

    with ExitStack() as ctx:
        def sb(name, shape, dtype=F32):
            return ctx.enter_context(nc.sbuf_tensor(name, shape, dtype))

        def bank(name):
            return ctx.enter_context(nc.psum_tensor(name, [P, 512], F32))

        def sem(name):
            return ctx.enter_context(nc.semaphore(name))

        const = sb("const", [P, NCONST])
        x_tok = sb("x_tok", [P, TILES, C])
        aff = sb("aff", [C + 1, 2 * C + 3 * S + E])
        w_in_s = aff[0:C, 0:C]
        w_out_s = aff[:, C:2 * C]
        w_om = aff[:, 2 * C:2 * C + 3 * S]
        w_r = aff[:, 2 * C + 3 * S:]
        dw_high = sb("dw_high", [P, K2, C], F16)
        dw_low = sb("dw_low", [C, K2, C], F16)
        w_in_high = sb("w_in_high", [P, C], F16)
        w_in_low = sb("w_in_low", [C, C], F16)
        bias_raw = sb("bias_raw", [1, 2, C])
        bias = sb("bias", [BR, 2, C], F16)
        ones = sb("ones", [BR, P], F16)
        inside = sb("inside", [BR, H, CELLS], F16)
        vec = sb("vec", [C, 2 + E + E * (C + 1)])
        gam = vec[:, 0:1]
        bet = vec[:, 1:2]
        lng_t = vec[:, 2:2 + E]
        lnb_col = vec[:, 2 + E:].rearrange("c (e m) -> c e m", e=E)
        w1_high = sb("w1_high", [P, E * HID], F16)
        w1_low = sb("w1_low", [NR, E * HID], F16)
        w2_s = sb("w2_s", [P, E * HC, C])
        b2_bc = sb("b2_bc", [P, E * C])
        ident = const[:, CI["ident"][0]:CI["ident"][1]]
        before = const[:, CI["before"][0]:CI["before"][1]]
        mhalf = const[:, CI["mhalf"][0]:CI["mhalf"][1]]
        pix = const[:, CI["pix"][0]:CI["pix"][1]].unsqueeze(1)
        loc = const[:, CI["loc"][0]:CI["loc"][1]].unsqueeze(1)
        thr = const[:, CI["thr"][0]:CI["thr"][1]].unsqueeze(1)
        ubase = const[:, CI["ubase"][0]:CI["ubase"][1]].rearrange("p (q k g) -> p q k g", q=Q, g=2)
        vbase = [const[:, CI["vbase"][0] + h * S:CI["vbase"][0] + (h + 1) * S]
                 .rearrange("p (q k g) -> p q k g", q=Q, g=2) for h in range(2)]

        ln_sum = [sb(f"ln_sum{n}", [P, TP]) for n in range(4)]
        ln_mean = [sb(f"ln_mean{n}", [P, TP]) for n in range(4)]
        ln_ss = [sb(f"ln_ss{n}", [P, TP]) for n in range(4)]
        ln_var = [sb(f"ln_var{n}", [P, TP]) for n in range(4)]
        ln_rstd = [sb(f"ln_rstd{n}", [P, TP]) for n in range(4)]
        ln_xc = [sb(f"ln_xc{n}", [P, TP, C]) for n in range(4)]
        ln_sq = sb("ln_sq", [P, TP, C])

        x_in = sb("x_in", [P, TP, C])
        xn = sb("xn", [P, TP, C])
        xpad = sb("xpad", [P, 3, 2, H + 2, W], F16)
        x1n = sb("x1n", [P, TP, C])
        x1_t = sb("x1_t", [C + 1, TP * P])
        v_hi = sb("v_hi", [P, B, Q, GC, 2, LOC], F16)
        v_lo = sb("v_lo", [P, B, Q, GC, 2, LOC], F16)
        u = sb("u", [P, TP, S])
        v = sb("v", [P, TP, S])
        mx = sb("mx", [P, TP, G])
        es = sb("es", [P, TP, S])
        ex = es
        esum = sb("esum", [P, TP * Q, 2])
        rsum = sb("rsum", [P, TP * Q, 2])
        mask = es[:].rearrange("p t s -> p (t s)")
        past = sb("past", [P, TP * S, CELLS + 1])
        cell = sb("cell", [P, TP * S])
        uloc = cell
        dl = sb("dl", [P, TP * S, LOC])
        dv = [sb(f"dv{r}", [P, S, H]) for r in range(DR)]
        onehot = sb("onehot", [P, 2, TP * S, CELLS])
        hat_y = sb("hat_y", [P, 2, TP * S, H])
        hat_part = hat_y[:].rearrange("p o s y -> p o (s y)").bitcast(F16).rearrange("p o (n h) -> p o n h", h=2)
        wx = sb("wx", [P, 2, TP * NP, 2 * LOC])
        wk = [sb(f"wk{r}", [P, SC, H, CELLS]) for r in range(2)]
        wk_t = [sb(f"wk_t{r}", [P, TR, P]) for r in range(3)]
        prod = [sb(f"prod{r}", [P, NP, GC, 2 * LOC]) for r in range(2)]
        dw_bc, dw_h, dw_l = (prod[0][:, :, :, :].rearrange("p n c l -> p (n c l)")[:, i * K2 * C:(i + 1) * K2 * C]
                             .rearrange("p (k c) -> p k c", c=C) for i in range(3))
        samp = sb("samp", [P, TP, G, GC])
        samp_t = sb("samp_t", [C + 1, TP * P])
        x2 = sb("x2", [P, TP, C])
        out_s = x_tok
        z = sb("z", [P, TP, C])
        zn = sb("zn", [P, TP, C])
        z_t = samp_t
        zn_both = sb("zn_both", [P, TP * P], F16)
        zn_high = sb("zn_high", [NR, TP * P], F16)
        lg = sb("lg", [P, TP, E])
        lmax = sb("lmax", [P, TP])
        le = sb("le", [P, TP, E])
        lx = sb("lx", [P, TP, E])
        cmp_gt = sb("cmp_gt", [P, TP, E, E])
        cmp_eq = sb("cmp_eq", [P, TP, E, E])
        rank = sb("rank", [P, TP, E])
        rank_eq = sb("rank_eq", [P, TP, E])
        top = sb("top", [P, TP, E])
        ptop = sb("ptop", [P, TP, E])
        psm = sb("psm", [P, TP])
        prs = sb("prs", [P, TP])
        wexp = sb("wexp", [P, TP, E])
        h_all = sb("h_all", [P, HR, HC, 2 * P])
        h_t = [h_all[:, r, :, :] for r in range(HR)]
        w1_raw = h_all[0:C, :, :, :].rearrange("p r a n -> p (r a n)")
        bias_1 = h_all[C:C + 1, :, :, :].rearrange("p r a n -> p (r a n)")
        y_sb = sb("y_sb", [P, E // 2, 2 * P])
        yb = sb("yb", [P, 2 * E, C])
        ysum = sb("ysum", [P, 2, C])

        tr_ps = [bank(f"tr_ps{r}") for r in range(2)]
        ga_ps = [bank(f"ga_ps{r}") for r in range(2)]
        m_ps = [bank(f"m_ps{r}") for r in range(4)]

        s_x = sem("s_x")
        s_x_rest = sem("s_x_rest")
        s_tab = sem("s_tab")
        s_wa = sem("s_wa")
        s_wd = sem("s_wd")
        s_zero = sem("s_zero")
        s_full = sem("s_full")
        s_dwd = sem("s_dwd")
        s_lnb_ps = sem("s_lnb_ps")
        s_bias = sem("s_bias")
        s_w1s = sem("s_w1s")
        s_w1h = sem("s_w1h")
        s_w1 = sem("s_w1")
        s_znl = sem("s_znl")
        s_chain = sem("s_chain")
        s_var = [sem(f"s_var{n}") for n in range(4)]
        s_rstd = [sem(f"s_rstd{n}") for n in range(4)]
        s_xn = sem("s_xn")
        s_xnT = sem("s_xnT")
        s_xhi = sem("s_xhi")
        s_xpad = sem("s_xpad")
        s_conv = sem("s_conv")
        s_vps = sem("s_vps")
        s_vblk = sem("s_vblk")
        s_conv_rd = sem("s_conv_rd")
        s_x1n = sem("s_x1n")
        s_x1nT = sem("s_x1nT")
        s_x1t = sem("s_x1t")
        s_om = sem("s_om")
        s_es = sem("s_es")
        s_ex = sem("s_ex")
        s_dl = sem("s_dl")
        s_dv = sem("s_dv")
        s_absl = sem("s_absl")
        s_absv = sem("s_absv")
        s_hx = sem("s_hx")
        s_haty = sem("s_haty")
        s_hat = sem("s_hat")
        s_hlo = sem("s_hlo")
        s_vlo = sem("s_vlo")
        s_win = sem("s_win")
        s_ysb = sem("s_ysb")
        s_yt = sem("s_yt")
        s_oneh = sem("s_oneh")
        s_wx = sem("s_wx")
        s_wk = sem("s_wk")
        s_tr = sem("s_tr")
        s_wkt = sem("s_wkt")
        s_ga = sem("s_ga")
        s_ga_rd = sem("s_ga_rd")
        s_samp = sem("s_samp")
        s_sT = sem("s_sT")
        s_st = sem("s_st")
        s_proj = sem("s_proj")
        s_x2 = sem("s_x2")
        s_z = sem("s_z")
        s_zn = sem("s_zn")
        s_zT = sem("s_zT")
        s_znT = sem("s_znT")
        s_zt = sem("s_zt")
        s_znt = sem("s_znt")
        s_lg = sem("s_lg")
        s_lg_rd = sem("s_lg_rd")
        s_le = sem("s_le")
        s_lx = sem("s_lx")
        s_h = sem("s_h")
        s_ht = sem("s_ht")
        s_y_mm = sem("s_y_mm")
        s_y_rd = sem("s_y_rd")
        s_out = sem("s_out")
        s_st_out = sem("s_st_out")

        N_X, N_TAB, N_WA, N_WD = 16, 16, 16 * 4, 16 * 4

        block = ctx.enter_context(nc.Block())

        @block.sync
        def _(sp):
            sp.dma_start(x_tok[:, 0:TP, :], x_d[:, 0:TP, :]).then_inc(s_x, 16)
            sp.dma_start(const[:], table).then_inc(s_tab, 16)
            sp.dma_start(dw_bc.rearrange("p k c -> p (k c)"), taps.to_broadcast([P, K2 * C])).then_inc(s_wa, 16)
            sp.dma_start(aff[:], affine).then_inc(s_wa, 16)
            sp.dma_start(vec[:], vectors).then_inc(s_wa, 16)
            sp.dma_start(bias_raw[:].rearrange("o n c -> o (n c)"), biases).then_inc(s_wa, 16)
            sp.dma_start(x_tok[:, TP:TILES, :], x_d[:, TP:TILES, :]).then_inc(s_x_rest, 16)
            sp.dma_start(w1_raw, W1).then_inc(s_wd, 16)
            sp.dma_start(bias_1, b1).then_inc(s_wd, 16)
            sp.dma_start(w2_s[:].rearrange("p a c -> p (a c)"), W2).then_inc(s_wd, 16)
            sp.dma_start(b2_bc[:], b2.to_broadcast([P, E * C])).then_inc(s_wd, 16)
            with sp.Fori(0, B) as b:
                sp.wait_ge(s_out, b + 1)
                sp.dma_start(out_d[:, bass.ds(2 * b, 2), :], out_s[:, bass.ds(2 * b, 2), :]).then_inc(s_st_out, 16)
            sp.wait_ge(s_st_out, 16 * B)

        @block.gpsimd
        def _(pool):
            pool.memset(xpad[:], 0.0)
            pool.memset(bias[:], 0.0)
            pool.memset(ones[:], 1.0)
            pool.memset(inside[:, :, 1:CELLS], 1.0)
            pool.memset(inside[:, :, 0:1], 0.0).then_inc(s_zero, 1)
            pool.wait_ge(s_tab, N_TAB)
            pool.wait_ge(s_var[0], 1)
            pool.tensor_tensor(ln_rstd[0][:], ln_var[0][:], mhalf, ALU.pow).then_inc(s_rstd[0], 1)
            pool.memset(v_hi[:], 0.0)
            pool.memset(v_lo[:], 0.0)
            pool.memset(past[:, :, 0:1], 1.0)
            pool.memset(past[:, :, CELLS:CELLS + 1], 0.0).then_inc(s_full, 1)
            pool.wait_ge(s_full, 1)
            pool.memset(x1_t[C:C + 1, :], 1.0)
            pool.memset(samp_t[C:C + 1, :], 1.0)
            pool.memset(zn_high[C:NR, :], Z_SCALE)
            pool.memset(w1_low[C:NR, :], 0.0).then_inc(s_zero, 1)
            pool.wait_ge(s_zero, 2)

            def rstd(n, count):
                pool.wait_ge(s_var[n], count)
                pool.tensor_tensor(ln_rstd[n][:], ln_var[n][:], mhalf, ALU.pow).then_inc(s_rstd[n], 1)

            def hat_low(a, t):
                pool.wait_ge(s_haty, TP * a + t + 1)
                words = hat_part[:, bass.ds(a % 2, 1), t * (S * H):(t + 1) * (S * H), :]
                pool.tensor_tensor(words[:, :, :, 0].rearrange("p o n -> p (o n)"), dv[t % DR][:].rearrange("p s y -> p (s y)"),
                                   words[:, :, :, 1].rearrange("p o n -> p (o n)"), ALU.subtract).then_inc(s_hlo, 1)

            def body(j, has_a, has_d):
                for c in range(TP * WC):
                    if c % WC == 0:
                        pool.wait_ge(s_hlo, TP * j + c // WC + 1)
                    if c == 0:
                        pool.wait_ge(s_oneh, j + 1)
                    if c >= 2 or not first(j):
                        pool.wait_ge(s_tr, j * (TP * NG) + (c - 1) * (NG // WC))
                    pool.tensor_tensor(wk[c % 2][:],
                                       hat_y[:, bass.ds(j % 2, 1), c * SC:(c + 1) * SC, :].rearrange("p o s y -> p (o s) y")
                                       .unsqueeze(3).to_broadcast([P, SC, H, CELLS]),
                                       onehot[:, bass.ds(j % 2, 1), c * SC:(c + 1) * SC, :].rearrange("p o s y -> p (o s) y")
                                       .unsqueeze(2).to_broadcast([P, SC, H, CELLS]),
                                       ALU.mult).then_inc(s_wk, 1)
                    if c == POOL_AT["rstd0"] and has_a:
                        rstd(0, j + 2)
                    if c == POOL_AT["rstd2"] and has_d:
                        rstd(2, j)
                    if c == POOL_AT["rstd1"] and has_a:
                        rstd(1, j + 2)
                    if c == POOL_AT["rstd3"] and has_d:
                        rstd(3, j)
                    for t in range(TP):
                        if (t >= AHEAD or has_a) and c == POOL_AT["hat_low"][t]:
                            hat_low(j if t >= AHEAD else j + 1, t)

            rstd(1, 1)
            for t in range(AHEAD):
                hat_low(0, t)
            body(0, True, False)
            with pool.Fori(1, PAIRS - 1) as j:
                body(j, True, True)
            body(PAIRS - 1, False, True)
            rstd(2, PAIRS)
            rstd(3, PAIRS)

        @block.vector
        def _(dve):
            chain = [0, 0]

            def link(ins):
                chain[1] += 1
                ins.then_inc(s_chain, 1)
                dve.wait_ge(s_chain, chain[0] + chain[1])

            def moments(n, src, eps, read=None):
                link(dve.tensor_reduce(ln_sum[n][:], src, axis=AX.X, op=ALU.add))
                link(dve.tensor_scalar(ln_mean[n][:], ln_sum[n][:], 1.0 / C, None, ALU.mult))
                ins = dve.tensor_tensor(ln_xc[n][:], src, ln_mean[n][:].unsqueeze(2).to_broadcast([P, TP, C]), ALU.subtract)
                if read is None:
                    link(ins)
                else:
                    ins.then_inc(read[0], 1)
                    dve.wait_ge(read[0], read[1])
                link(dve.tensor_tensor(ln_sq[:], ln_xc[n][:], ln_xc[n][:], ALU.mult))
                link(dve.tensor_reduce(ln_ss[n][:], ln_sq[:], axis=AX.X, op=ALU.add))
                dve.tensor_scalar(ln_var[n][:], ln_ss[n][:], 1.0 / C, eps, ALU.mult, ALU.add).then_inc(s_var[n], 1)

            def normalise(n, dst, count, done):
                dve.wait_ge(s_rstd[n], count)
                dve.tensor_tensor(dst, ln_xc[n][:], ln_rstd[n][:].unsqueeze(2).to_broadcast([P, TP, C]),
                                  ALU.mult).then_inc(done, 1)

            def input_moments(a):
                link(dve.tensor_copy(x_in[:], x_tok[:, bass.ds(a * TP, TP), :]))
                moments(0, x_in[:], 1e-6)

            def input_low(a):
                dve.wait_ge(s_xhi, a + 1)
                src = m_ps[0][0:C, :].rearrange("c (i y x) -> c i y x", i=2, y=H)
                for dx in range(3):
                    lo, hi = max(0, 1 - dx), min(W, W + 1 - dx)
                    ins = dve.tensor_tensor(xpad[C:P, dx, :, 1:H + 1, lo:hi], src[:, :, :, lo + dx - 1:hi + dx - 1],
                                            xpad[0:C, dx, :, 1:H + 1, lo:hi], ALU.subtract)
                ins.then_inc(s_xpad, 1)

            def conv_moments(a):
                dve.wait_ge(s_conv, a + 1)
                moments(1, m_ps[2][:, 0:TP * C].rearrange("p (t c) -> p t c", c=C), 1e-6 * TAP_SCALE ** 2, (s_conv_rd, a + 1))

            def om_tile(t):
                return m_ps[2 + t // 2][:, 256 * (t % 2):256 * (t % 2) + 3 * S]

            def image_low(a):
                dve.wait_ge(s_vblk, a + 1)
                for i in range(2):
                    for g in range(2):
                        src = m_ps[3 - 3 * i][g * KC:(g + 1) * KC, 0:LOC * C].rearrange("p (l q g c) -> p g q c l", l=LOC, q=Q, g=2)
                        lo, hi = (v[g * KC:(g + 1) * KC, bass.ds(2 * a + i, 1), :, :, g, :]
                                  .rearrange("p o q c l -> p (o q) c l") for v in (v_lo, v_hi))
                        ins = dve.tensor_tensor(lo, src[:, g, :, :, :], hi, ALU.subtract)
                ins.then_inc(s_vlo, 1)

            def coordinates(a):
                dve.wait_ge(s_om, a + 1)
                for t in range(TP):
                    off = om_tile(t)[:, 0:2 * S].rearrange("p (q g k o) -> p q k g o", q=Q, g=2, k=K2)
                    ins = dve.tensor_tensor(v[:, t, :].rearrange("p (q k g) -> p q k g", q=Q, g=2), off[:, :, :, :, 1],
                                            vbase[t % 2], ALU.add)
                if first(a):
                    link(ins)
                    row_distance(a, 0)
                for t in range(TP):
                    off = om_tile(t)[:, 0:2 * S].rearrange("p (q g k o) -> p q k g o", q=Q, g=2, k=K2)
                    dve.tensor_tensor(u[:, t, :].rearrange("p (q k g) -> p q k g", q=Q, g=2), off[:, :, :, :, 0],
                                      ubase, ALU.add)
                    ins = dve.tensor_reduce(mx[:, t, :], om_tile(t)[:, 2 * S:3 * S].rearrange("p (g k) -> p g k", k=K2),
                                            axis=AX.X, op=ALU.max)
                link(ins)
                for t in range(TP):
                    ins = dve.tensor_tensor(es[:, t, :].rearrange("p (q k g) -> p q k g", q=Q, g=2),
                                            om_tile(t)[:, 2 * S:3 * S].rearrange("p (q g k) -> p q k g", q=Q, g=2),
                                            mx[:, t, :].rearrange("p (q g) -> p q g", g=2).unsqueeze(2)
                                            .to_broadcast([P, Q, K2, 2]), ALU.subtract)
                ins.then_inc(s_es, 1)

            def one_hots(a):
                uf = u[:].rearrange("p t s -> p (t s)").unsqueeze(2)
                link(dve.tensor_tensor(past[:, :, 1:CELLS], uf.to_broadcast([P, TP * S, CELLS - 1]),
                                       thr.to_broadcast([P, TP * S, CELLS - 1]), ALU.is_ge))
                if not first(a):
                    dve.wait_ge(s_wk, (a - 1) * (TP * WC))
                dve.tensor_tensor(onehot[:, bass.ds(a % 2, 1), :, :].rearrange("p o s c -> p (o s) c"), past[:, :, 0:CELLS],
                                  past[:, :, 1:CELLS + 1], ALU.subtract).then_inc(s_oneh, 1)

            def distances(a):
                link(dve.tensor_reduce(cell[:], past[:, :, 1:CELLS], axis=AX.X, op=ALU.add))
                link(dve.scalar_tensor_tensor(uloc[:], cell[:], -4.0, u[:].rearrange("p t s -> p (t s)"),
                                              ALU.mult, ALU.add))
                dve.tensor_tensor(dl[:], uloc[:].unsqueeze(2).to_broadcast([P, TP * S, LOC]),
                                  loc.to_broadcast([P, TP * S, LOC]), ALU.subtract).then_inc(s_dl, 1)

            def row_distance(a, t):
                if t >= DR or not first(a):
                    last_use = t - DR if t >= DR else t - TP if t > 0 else -1
                    dve.wait_ge(s_hlo, TP * a + last_use + 1)
                dve.tensor_tensor(dv[t % DR][:], v[:, t, :].unsqueeze(2).to_broadcast([P, S, H]),
                                  pix.to_broadcast([P, S, H]), ALU.subtract).then_inc(s_dv, 1)

            def tap_weights(a):
                dve.wait_ge(s_ex, a + 1)
                exv = ex[:].rearrange("p t (q k g) -> p (t q) k g", q=Q, g=2)
                link(dve.tensor_reduce(esum[:], exv.rearrange("p q k g -> p q g k"), axis=AX.X, op=ALU.add))
                link(dve.reciprocal(rsum[:], esum[:]))
                link(dve.tensor_tensor(mask.rearrange("p (q k g) -> p q k g", k=K2, g=2), exv,
                                       rsum[:].unsqueeze(2).to_broadcast([P, TP * Q, K2, 2]), ALU.mult))
                dve.wait_ge(s_hx, a + 1)
                dve.tensor_tensor(wx[:, bass.ds(a % 2, 1), :, :].rearrange("p o n (g l) -> p (o n g) l", l=LOC),
                                  dl[:], mask.unsqueeze(2).to_broadcast([P, TP * S, LOC]),
                                  ALU.mult).then_inc(s_wx, 1)

            def weigh(j, t, n):
                dve.wait_ge(s_ga, j * (TP * NG) + t * NG + -(-(n + 1) * PB // TR))
                dve.tensor_tensor(
                    prod[t % 2][:, n * PB:(n + 1) * PB, :, :],
                    ga_ps[n % 2][:, 0:PB * NV].rearrange("p (n c l) -> p n c l", n=PB, c=GC),
                    wx[:, bass.ds(j % 2, 1), t * NP + n * PB:t * NP + (n + 1) * PB, :].rearrange("p o n l -> p (o n) l")
                    .unsqueeze(2).to_broadcast([P, PB, GC, 2 * LOC]), ALU.mult).then_inc(s_ga_rd, 1)

            def tap_sum(j, t, q):
                dve.wait_ge(s_ga_rd, j * (TP * NBK) + t * NBK + TAP_SUM_AT[q] + 1)
                if t == 0 and q == 0 and not first(j):
                    dve.wait_ge(s_sT, j)
                ins = dve.tensor_reduce(
                    samp[:, t, 2 * q:2 * q + 2, :],
                    prod[t % 2][:, q * K2:(q + 1) * K2, :, :].rearrange("p k c (g l) -> p g c k l", g=2),
                    axis=AX.XY, op=ALU.add)
                if t == TP - 1 and q == Q - 1:
                    ins.then_inc(s_samp, 1)

            def add_bias_1(q):
                n = slice(q * 512, (q + 1) * 512)
                dve.wait_ge(s_lnb_ps, q + 1)
                dve.tensor_tensor(bias_1[:, n], m_ps[1][C:C + 1, :], bias_1[:, n], ALU.add).then_inc(s_bias, 1)

            def scale_w1():
                dve.wait_ge(s_lnb_ps, HR)
                for e in range(E):
                    ins = dve.tensor_scalar(w1_raw[:, e * HID:(e + 1) * HID], w1_raw[:, e * HID:(e + 1) * HID],
                                            lng_t[:, e:e + 1], W1_SCALE, ALU.mult, ALU.mult)
                ins.then_inc(s_w1s, 1)

            def low_w1():
                dve.wait_ge(s_w1h, 3)
                dve.wait_ge(s_bias, HR)
                dve.tensor_tensor(w1_low[0:C, :], w1_raw, w1_high[0:C, :], ALU.subtract)
                dve.scalar_tensor_tensor(w1_low[NR - 1:NR, :], bias_1, W1_SCALE, w1_low[C:C + 1, :],
                                         ALU.mult, ALU.subtract).then_inc(s_w1, 1)

            def residual(d, weighed=None):
                dve.wait_ge(s_proj, d + 1)
                if last(d):
                    dve.wait_ge(s_out, 2 * d)
                else:
                    dve.wait_ge(s_ga_rd, weighed)
                dve.tensor_tensor(x2[:], m_ps[1][:, 0:TP * C].rearrange("p (t c) -> p t c", c=C),
                                  x_tok[:, bass.ds(d * TP, TP), :], ALU.add).then_inc(s_x2, 1)
                dve.wait_ge(s_x2, d + 1)
                moments(2, x2[:], 1e-5)

            def inner_norm(d):
                normalise(2, z[:], d + 1, s_z)
                dve.wait_ge(s_z, d + 1)
                moments(3, z[:], 1e-5)

            def zn_low(d):
                dve.wait_ge(s_znt, d + 1)
                dve.scalar_tensor_tensor(zn_both[C:P, :], m_ps[0][0:C, :], Z_SCALE, zn_both[0:C, :],
                                         ALU.mult, ALU.subtract).then_inc(s_znl, 1)

            def route(d):
                dve.wait_ge(s_lg, d + 1)
                dve.tensor_copy(lg[:], m_ps[1][:, 0:TP * E].rearrange("p (t e) -> p t e", e=E)).then_inc(s_lg_rd, 1)
                dve.wait_ge(s_lg_rd, d + 1)
                link(dve.tensor_reduce(lmax[:], lg[:], axis=AX.X, op=ALU.max))
                dve.tensor_tensor(le[:], lg[:], lmax[:].unsqueeze(2).to_broadcast([P, TP, E]),
                                  ALU.subtract).then_inc(s_le, 1)
                for t in range(TP):
                    other = lg[:, t, :].unsqueeze(1).to_broadcast([P, E, E])
                    own = lg[:, t, :].unsqueeze(2).to_broadcast([P, E, E])
                    dve.tensor_tensor(cmp_gt[:, t, :, :], other, own, ALU.is_gt)
                    ins = dve.tensor_tensor(cmp_eq[:, t, :, :], other, own, ALU.is_equal)
                link(ins)
                link(dve.tensor_tensor(cmp_eq[:].rearrange("p t i j -> p t (i j)"), cmp_eq[:].rearrange("p t i j -> p t (i j)"),
                                       before.unsqueeze(1).to_broadcast([P, TP, E * E]), ALU.mult))
                dve.tensor_reduce(rank[:], cmp_gt[:], axis=AX.X, op=ALU.add)
                link(dve.tensor_reduce(rank_eq[:], cmp_eq[:], axis=AX.X, op=ALU.add))
                link(dve.tensor_tensor(rank[:], rank[:], rank_eq[:], ALU.add))
                link(dve.tensor_scalar(top[:], rank[:], 2.0, None, ALU.is_lt))

            def expert_weights(d):
                dve.wait_ge(s_lx, d + 1)
                link(dve.tensor_tensor(ptop[:], lx[:], top[:], ALU.mult))
                link(dve.tensor_reduce(psm[:], ptop[:], axis=AX.X, op=ALU.add))
                link(dve.reciprocal(prs[:], psm[:]))
                link(dve.tensor_tensor(wexp[:], ptop[:], prs[:].unsqueeze(2).to_broadcast([P, TP, E]), ALU.mult))

            def outputs_in(d, i):
                dve.wait_ge(s_yt, 2 * d + i + 1)
                for t in range(2):
                    ins = dve.tensor_tensor(yb[:, t * E:(t + 1) * E, :],
                                            m_ps[2 + t][:, :].rearrange("p (e c) -> p e c", c=C),
                                            b2_bc[:].rearrange("p (e c) -> p e c", c=C), ALU.add)
                ins.then_inc(s_y_rd, 1)

            def combine(d, i):
                dve.wait_ge(s_y_rd, 2 * d + i + 1)
                wv = wexp[:, 2 * i:2 * i + 2, :].rearrange("p t e -> p (t e)").unsqueeze(2)
                link(dve.tensor_tensor(yb[:], yb[:],
                                       wv.to_broadcast([P, 2 * E, C]), ALU.mult))
                link(dve.tensor_reduce(ysum[:], yb[:].rearrange("p (t e) c -> p t c e", e=E), axis=AX.X, op=ALU.add))
                dve.tensor_tensor(out_s[:, bass.ds(d * TP + 2 * i, 2), :], ysum[:], x2[:, 2 * i:2 * i + 2, :], ALU.add).then_inc(s_out, 1)

            def body(j, has_a, has_d):
                dve.wait_ge(s_wx, j + 1)
                for m in range(TP * NBK):
                    if has_a:
                        if m == DVE_AT["input_moments"]:
                            input_moments(j + 1)
                        if m == DVE_AT["input_norm"]:
                            normalise(0, xn[:], j + 2, s_xn)
                        if m == DVE_AT["input_low"]:
                            input_low(j + 1)
                        if m == DVE_AT["conv_moments"]:
                            conv_moments(j + 1)
                        if m == DVE_AT["image_low"]:
                            image_low(j + 1)
                        if m == DVE_AT["conv_norm"]:
                            normalise(1, x1n[:], j + 2, s_x1n)
                        if m == DVE_AT["coordinates"]:
                            coordinates(j + 1)
                        if m == DVE_AT["one_hots"]:
                            one_hots(j + 1)
                        if m == DVE_AT["distances"]:
                            distances(j + 1)
                        if m == DVE_AT["tap_weights"]:
                            tap_weights(j + 1)
                    if has_d:
                        if m == DVE_AT["residual"]:
                            residual(j - 1, j * (TP * NBK) + m)
                        if m == DVE_AT["inner_norm"]:
                            inner_norm(j - 1)
                        if m == DVE_AT["zn_norm"]:
                            normalise(3, zn[:], j, s_zn)
                        if m == DVE_AT["zn_low"]:
                            zn_low(j - 1)
                        if m == DVE_AT["route"]:
                            route(j - 1)
                        if m == DVE_AT["expert_weights"]:
                            expert_weights(j - 1)
                        if m == DVE_AT["outputs_in"][0]:
                            outputs_in(j - 1, 0)
                        if m == DVE_AT["combine"][0]:
                            combine(j - 1, 0)
                    for t in range(TP):
                        if (t >= AHEAD or has_a) and m == DVE_AT["row_distance"][t]:
                            row_distance(j if t >= AHEAD else j + 1, t)
                    if first(j):
                        for q in range(HR):
                            if m == DVE_AT["bias_1"][q]:
                                add_bias_1(q)
                        if m == DVE_AT["w1_scale"]:
                            scale_w1()
                        if m == DVE_AT["w1_low"]:
                            low_w1()
                    weigh(j, m // NBK, m % NBK)
                    for q in range(Q):
                        if m % NBK == TAP_SUM_AT[q]:
                            tap_sum(j, m // NBK, q)
                    if has_d and m == DVE_AT["outputs_in"][1]:
                        outputs_in(j - 1, 1)
                    if has_d and m == DVE_AT["combine"][1]:
                        combine(j - 1, 1)

            dve.wait_ge(s_x, N_X)
            input_moments(0)
            dve.wait_ge(s_tab, N_TAB)
            dve.wait_ge(s_wa, N_WA)
            dve.tensor_scalar(dw_h, dw_bc, TAP_SCALE, None, ALU.mult)
            dve.tensor_scalar(bias_raw[:, 0, :], bias_raw[:, 0, :], TAP_SCALE, None, ALU.mult)
            link(dve.tensor_scalar(bias_raw[:, 1, :], bias_raw[:, 1, :], V_SCALE, None, ALU.mult))
            for half in range(2):
                rows = slice(half * C, (half + 1) * C)
                dve.tensor_tensor(dw_high[rows, :, :], ident[rows, rows].unsqueeze(1).to_broadcast([C, K2, C]),
                                  dw_h[rows, :, :], ALU.mult)
            dve.wait_ge(s_zero, 1)
            link(dve.tensor_copy(bias[0:1, :, :], bias_raw[:]))
            dve.tensor_tensor(dw_l[0:C, :, :], ident[0:C, 0:C].unsqueeze(1).to_broadcast([C, K2, C]),
                              dw_h[0:C, :, :], ALU.mult)
            normalise(0, xn[:], 1, s_xn)
            dve.wait_ge(s_win, 1)
            dve.scalar_tensor_tensor(w_in_low[:], w_in_s, V_SCALE, w_in_high[0:C, :], ALU.mult, ALU.subtract)
            link(dve.tensor_tensor(bias[BR - 1:BR, :, :], bias_raw[:], bias[0:1, :, :], ALU.subtract))
            dve.tensor_tensor(dw_low[:], dw_l[0:C, :, :], dw_high[0:C, :, :], ALU.subtract).then_inc(s_dwd, 1)
            input_low(0)
            conv_moments(0)
            dve.wait_ge(s_zero, 2)
            image_low(0)
            normalise(1, x1n[:], 1, s_x1n)
            coordinates(0)
            one_hots(0)
            distances(0)
            for t in range(1, AHEAD):
                row_distance(0, t)
            tap_weights(0)
            dve.wait_ge(s_x_rest, N_X)

            body(0, True, False)
            before_loop, chain[1] = chain[1], 0
            with dve.Fori(1, PAIRS - 1) as j:
                chain[0] = (j - 1) * LINKS + before_loop
                body(j, True, True)
            assert chain[1] == LINKS, chain[1]
            chain[0], chain[1] = before_loop + (PAIRS - 2) * LINKS, 0
            body(PAIRS - 1, False, True)
            residual(PAIRS - 1)
            inner_norm(PAIRS - 1)
            normalise(3, zn[:], PAIRS, s_zn)
            zn_low(PAIRS - 1)
            route(PAIRS - 1)
            expert_weights(PAIRS - 1)
            for i in range(2):
                outputs_in(PAIRS - 1, i)
                combine(PAIRS - 1, i)

        @block.scalar
        def _(act):
            act.wait_ge(s_wa, N_WA)
            for half in range(2):
                ins = act.activation(w_in_high[half * C:(half + 1) * C, :], w_in_s, ACT.Copy, scale=V_SCALE)
            ins.then_inc(s_win, 1)
            act.wait_ge(s_zero, 1)

            def pad_image(a):
                act.wait_ge(s_xnT, a + 1)
                if not first(a):
                    act.wait_ge(s_vps, a)
                    act.wait_ge(s_conv, a)
                src = m_ps[0][0:C, :].rearrange("c (i y x) -> c i y x", i=2, y=H)
                for dx in range(3):
                    lo, hi = max(0, 1 - dx), min(W, W + 1 - dx)
                    ins = act.copy(xpad[0:C, dx, :, 1:H + 1, lo:hi], src[:, :, :, lo + dx - 1:hi + dx - 1])
                ins.then_inc(s_xhi, 1)

            def block_diagonal(a):
                act.wait_ge(s_vps, a + 1)
                for i in range(2):
                    for g in range(2):
                        src = m_ps[3 - 3 * i][g * KC:(g + 1) * KC, 0:LOC * C].rearrange("p (l q g c) -> p g q c l", l=LOC, q=Q, g=2)
                        ins = act.copy(v_hi[g * KC:(g + 1) * KC, bass.ds(2 * a + i, 1), :, :, g, :]
                                       .rearrange("p o q c l -> p (o q) c l"), src[:, g, :, :, :])
                ins.then_inc(s_vblk, 1)

            def conv_gelu(a):
                act.wait_ge(s_x1nT, a + 1)
                act.activation(x1_t[0:C, :], m_ps[3][0:C, :], ACT.Gelu, bias=bet, scale=gam).then_inc(s_x1t, 1)

            def tap_exp(a):
                act.wait_ge(s_es, a + 1)
                act.activation(ex[:], es[:], ACT.Exp).then_inc(s_ex, 1)

            def hat_x_abs(a):
                act.wait_ge(s_dl, a + 1)
                act.activation(dl[:], dl[:], ACT.Abs).then_inc(s_absl, 1)

            def hat_x(a):
                act.wait_ge(s_absl, a + 1)
                act.activation(dl[:], dl[:], ACT.Relu, bias=1.0 / (W_SCALE * V_SCALE), scale=-1.0 / (W_SCALE * V_SCALE)).then_inc(s_hx, 1)

            def row_abs(a, t):
                act.wait_ge(s_dv, a * TP + t + 1)
                act.activation(dv[t % DR][:], dv[t % DR][:], ACT.Abs).then_inc(s_absv, 1)

            def row_hat(a, t):
                act.wait_ge(s_absv, a * TP + t + 1)
                act.activation(dv[t % DR][:], dv[t % DR][:], ACT.Relu, bias=W_SCALE, scale=-W_SCALE).then_inc(s_hat, 1)

            def row_high(a, t):
                act.wait_ge(s_hat, a * TP + t + 1)
                if t == 0 and not first(a):
                    act.wait_ge(s_wk, (a - 1) * (TP * WC))
                act.copy(hat_part[:, bass.ds(a % 2, 1), t * (S * H):(t + 1) * (S * H), 1].rearrange("p o n -> p (o n)"),
                         dv[t % DR][:].rearrange("p s y -> p (s y)")).then_inc(s_haty, 1)

            def samples_out(d):
                act.wait_ge(s_sT, d + 1)
                act.copy(samp_t[0:C, :], m_ps[1][0:C, :]).then_inc(s_st, 1)

            def z_out(d):
                act.wait_ge(s_zT, d + 1)
                act.copy(z_t[0:C, :], m_ps[1][0:C, :]).then_inc(s_zt, 1)

            def zn_out(d):
                act.wait_ge(s_znT, d + 1)
                act.activation(zn_high[0:C, :], m_ps[0][0:C, :], ACT.Copy, scale=Z_SCALE)
                act.activation(zn_both[0:C, :], m_ps[0][0:C, :], ACT.Copy, scale=Z_SCALE).then_inc(s_znt, 1)

            def router_exp(d):
                act.wait_ge(s_le, d + 1)
                act.activation(lx[:], le[:], ACT.Exp).then_inc(s_lx, 1)

            def hidden(d, n):
                act.wait_ge(s_h, d * (2 * E) + n + 1)
                if n >= HR or last(d):
                    act.wait_ge(s_y_mm, d * (2 * E) + n - HR + 1)
                act.activation(h_t[n % HR][:].rearrange("p a n -> p (a n)"), m_ps[n % 2][:, :], ACT.Gelu,
                               scale=1.0 / (W1_SCALE * Z_SCALE)).then_inc(s_ht, 1)

            def high_w1(n):
                if n < 2:
                    act.wait_ge(s_w1s, 1)
                    act.copy(w1_high[n * C:(n + 1) * C, :], w1_raw).then_inc(s_w1h, 1)
                else:
                    act.wait_ge(s_bias, HR)
                    act.activation(w1_low[C:C + 1, :], bias_1, ACT.Copy, scale=W1_SCALE).then_inc(s_w1h, 1)

            def outputs_out(d, i):
                act.wait_ge(s_y_mm, d * (2 * E) + (i + 1) * E)
                if i == 1 or last(d):
                    act.wait_ge(s_yt, 2 * d + i)
                for b in range(2):
                    ins = act.copy(y_sb[:, 2 * b:2 * b + 2, :].rearrange("p e n -> p (e n)"), m_ps[2 + b][:, :])
                ins.then_inc(s_ysb, 1)

            def body(j, has_a, has_d):
                for n in range(TP * NG):
                    act.wait_ge(s_tr, j * (TP * NG) + n + 1)
                    if n >= 3 or not first(j):
                        act.wait_ge(s_ga, j * (TP * NG) + n - 2)
                    act.copy(wk_t[n % 3][:], tr_ps[n % 2][:, :].rearrange("p (n m) -> p n m", n=TR)).then_inc(s_wkt, 1)
                    if has_d:
                        if n == ACT_AT["samples_out"]:
                            samples_out(j - 1)
                        if n == ACT_AT["z_out"]:
                            z_out(j - 1)
                        if n == ACT_AT["router_exp"]:
                            router_exp(j - 1)
                        if n == ACT_AT["zn_out"]:
                            zn_out(j - 1)
                        for unit in range(2 * E):
                            if n == ACT_AT["hidden"][unit]:
                                hidden(j - 1, unit)
                        for i in range(2):
                            if n == ACT_AT["outputs_out"][i]:
                                outputs_out(j - 1, i)
                    if has_a:
                        if n == ACT_AT["pad_image"]:
                            pad_image(j + 1)
                        if n == ACT_AT["block_diagonal"]:
                            block_diagonal(j + 1)
                        if n == ACT_AT["conv_gelu"]:
                            conv_gelu(j + 1)
                        if n == ACT_AT["tap_exp"]:
                            tap_exp(j + 1)
                        if n == ACT_AT["hat_x_abs"]:
                            hat_x_abs(j + 1)
                        if n == ACT_AT["hat_x"]:
                            hat_x(j + 1)
                    for t in range(TP):
                        if t >= AHEAD or has_a:
                            a = j if t >= AHEAD else j + 1
                            if n == ACT_AT["row_abs"][t]:
                                row_abs(a, t)
                            if n == ACT_AT["row_hat"][t]:
                                row_hat(a, t)
                            if n == ACT_AT["row_high"][t]:
                                row_high(a, t)
                    if first(j):
                        for i in range(3):
                            if n == ACT_AT["w1_high"][i]:
                                high_w1(i)

            pad_image(0)
            act.wait_ge(s_zero, 2)
            block_diagonal(0)
            conv_gelu(0)
            row_abs(0, 0)
            row_hat(0, 0)
            row_high(0, 0)
            tap_exp(0)
            hat_x_abs(0)
            hat_x(0)
            for t in range(1, AHEAD):
                row_abs(0, t)
                row_hat(0, t)
                row_high(0, t)
            body(0, True, False)
            with act.Fori(1, PAIRS - 1) as j:
                body(j, True, True)
            body(PAIRS - 1, False, True)
            samples_out(PAIRS - 1)
            z_out(PAIRS - 1)
            zn_out(PAIRS - 1)
            router_exp(PAIRS - 1)
            for n in range(2 * E):
                if n == E:
                    outputs_out(PAIRS - 1, 0)
                hidden(PAIRS - 1, n)
            outputs_out(PAIRS - 1, 1)

        @block.tensor
        def _(pe):
            pe.wait_ge(s_tab, N_TAB)
            pe.wait_ge(s_wa, N_WA)

            def transposes(src, dst):
                for t in range(TP):
                    if t == 0:
                        ins = pe.transpose(dst[:, 0:P], src[:, 0:2, :].rearrange("p t c -> p (t c)"), ident)
                    else:
                        ins = pe.transpose(dst[0:C, t * P:(t + 1) * P], src[:, t, :], ident)
                return ins

            def input_t(a):
                pe.wait_ge(s_xn, a + 1)
                transposes(xn, m_ps[0]).then_inc(s_xnT, 1)

            def convolve(a):
                pe.wait_ge(s_xpad, a + 1)
                for t in range(TP):
                    y0 = (t % 2) * (H // 2)
                    acc = m_ps[2][:, t * C:(t + 1) * C]
                    for k in range(K2):
                        dy, dx = k // 3, k % 3
                        px = xpad[:, dx, t // 2, y0 + dy:y0 + dy + H // 2, :].rearrange("c y x -> c (y x)")
                        pe.matmul(acc, px, dw_high[:, k, :], start=(k == 0), stop=False)
                        pe.matmul(acc, px[0:C, :], dw_low[:, k, :], start=False, stop=False)
                    ins = pe.matmul(acc, ones[:], bias[:, 0, :], start=False, stop=True)
                ins.then_inc(s_conv, 1)

            def project_in(a):
                pe.wait_ge(s_xpad, a + 1)
                for i in range(2):
                    for l in range(LOC):
                        px = xpad[:, min(l, 1), i, 1:H + 1, :].rearrange("c y x -> c (y x)")[:, max(l - 1, 0)::CELLS]
                        there = (ones[:, 0:KC] if l else inside[:].rearrange("r y x -> r (y x)"))
                        for g in range(2):
                            acc = m_ps[3 - 3 * i][g * KC:(g + 1) * KC, l * C:(l + 1) * C]
                            pe.matmul(acc, px, w_in_high[:], start=True, stop=False)
                            pe.matmul(acc, px[0:C, :], w_in_low[:], start=False, stop=False)
                            ins = pe.matmul(acc, there, bias[:, 1, :], start=False, stop=True)
                ins.then_inc(s_vps, 1)

            def conv_t(a):
                pe.wait_ge(s_x1n, a + 1)
                pe.wait_ge(s_vlo, a + 1)
                transposes(x1n, m_ps[3]).then_inc(s_x1nT, 1)

            def offsets(a):
                pe.wait_ge(s_x1t, a + 1)
                for t in range(TP):
                    ins = pe.matmul(m_ps[2 + t // 2][:, 256 * (t % 2):256 * (t % 2) + 3 * S],
                                    x1_t[:, t * P:(t + 1) * P], w_om, start=True, stop=True)
                ins.then_inc(s_om, 1)

            def transpose_weights(j, n):
                e = n % NG
                per = NG // WC
                c = (n // NG) * WC + e // per
                if e % per == 0:
                    pe.wait_ge(s_wk, j * (TP * WC) + c + 1)
                if n >= 2 or not first(j):
                    pe.wait_ge(s_wkt, j * (TP * NG) + n - 1)
                src = wk[c % 2][:].rearrange("p (n g) y x -> p n (g y x)", g=2)
                for i in range(TR):
                    ins = pe.transpose(tr_ps[n % 2][:, i * P:(i + 1) * P], src[:, (e % per) * TR + i, :], ident)
                ins.then_inc(s_tr, 1)

            def gather(j, n):
                pe.wait_ge(s_wkt, j * (TP * NG) + n + 1)
                t, e = n // NG, n % NG
                for i in range(TR):
                    p = e * TR + i
                    bk = t * NBK + p // PB
                    if p % PB == 0 and (bk >= 2 or not first(j)):
                        pe.wait_ge(s_ga_rd, j * (TP * NBK) + bk - 1)
                    v_h, v_l = (v[:, bass.ds(2 * j + t // 2, 1), p // K2, :, :, :].rearrange("p b c g l -> p (b c g l)")
                                for v in (v_hi, v_lo))
                    w_l, w_h = (wk_t[n % 3][:, i, :].bitcast(F16)[:, h::2] for h in range(2))
                    for w, v, st, sp in ((w_h, v_h, True, False), (w_h, v_l, False, False), (w_l, v_h, False, True)):
                        ins = pe.matmul(ga_ps[bk % 2][:, (p % PB) * NV:(p % PB + 1) * NV], w, v, start=st, stop=sp)
                ins.then_inc(s_ga, 1)

            def samples_t(d):
                pe.wait_ge(s_samp, d + 1)
                transposes(samp[:].rearrange("p t g c -> p t (g c)"), m_ps[1]).then_inc(s_sT, 1)

            def project_out(d):
                pe.wait_ge(s_st, d + 1)
                for t in range(TP):
                    ins = pe.matmul(m_ps[1][:, t * C:(t + 1) * C], samp_t[:, t * P:(t + 1) * P], w_out_s,
                                    start=True, stop=True)
                ins.then_inc(s_proj, 1)

            def router_t(d):
                pe.wait_ge(s_z, d + 1)
                transposes(z, m_ps[1]).then_inc(s_zT, 1)

            def router(d):
                pe.wait_ge(s_zt, d + 1)
                for t in range(TP):
                    ins = pe.matmul(m_ps[1][:, t * E:(t + 1) * E], z_t[:, t * P:(t + 1) * P], w_r, start=True, stop=True)
                ins.then_inc(s_lg, 1)

            def experts_t(d, images):
                pe.wait_ge(s_vlo, images)
                pe.wait_ge(s_zn, d + 1)
                transposes(zn, m_ps[0]).then_inc(s_znT, 1)

            def bias_product(q):
                if q == 0:
                    pe.wait_ge(s_wd, N_WD)
                else:
                    pe.wait_ge(s_bias, q)
                for i in range(2):
                    e = 2 * q + i
                    ins = pe.matmul(m_ps[1][0:C + 1, i * HID:(i + 1) * HID], lnb_col[:, e, :],
                                    w1_raw[:, e * HID:(e + 1) * HID], start=True, stop=True)
                ins.then_inc(s_lnb_ps, 1)

            def expert_in(d, n):
                if n == 0:
                    pe.wait_ge(s_znl, d + 1)
                if n == 1:
                    pe.wait_ge(s_lg_rd, d + 1)
                if n >= 2:
                    pe.wait_ge(s_ht, d * (2 * E) + n - 1)
                i, e = n // E, n % E
                for a in range(HC):
                    c0 = e * HID + a * P
                    pe.matmul(m_ps[n % 2][:, a * 2 * P:(a + 1) * 2 * P], w1_high[:, c0:c0 + P],
                              zn_both[:, i * 2 * P:(i + 1) * 2 * P], start=True, stop=False)
                    ins = pe.matmul(m_ps[n % 2][:, a * 2 * P:(a + 1) * 2 * P], w1_low[:, c0:c0 + P],
                                    zn_high[:, i * 2 * P:(i + 1) * 2 * P], start=False, stop=True)
                ins.then_inc(s_h, 1)

            def expert_out(d, n, last_es):
                i, e = n // E, n % E
                pe.wait_ge(s_ht, d * (2 * E) + n + 1)
                if n == 0:
                    pe.wait_ge(s_es, last_es)
                if n == E:
                    pe.wait_ge(s_y_rd, 2 * d + 1)
                rows, c0 = (e % 2) * C, (e // 2 % 2) * 2 * P
                for a in range(HC):
                    ins = pe.matmul(m_ps[2 + e // 4][rows:rows + C, c0:c0 + 2 * P], w2_s[:, e * HC + a, :],
                                    h_t[n % HR][:, a, :], start=(a == 0), stop=(a == HC - 1))
                ins.then_inc(s_y_mm, 1)

            def outputs_t(d, i):
                pe.wait_ge(s_ysb, 2 * d + i + 1)
                for t in range(2):
                    for e in range(E // 2):
                        ins = pe.transpose(m_ps[2 + t][:, e * P:(e + 1) * P], y_sb[:, e, t * P:(t + 1) * P], ident)
                ins.then_inc(s_yt, 1)

            def body(j, has_a, has_d):
                for n in range(TP * NG):
                    transpose_weights(j, n)
                    if n > 0:
                        gather(j, n - 1)
                    elif not first(j):
                        gather(j - 1, TP * NG - 1)
                    if has_d:
                        if n == PE_AT["samples_t"]:
                            samples_t(j - 1)
                        if n == PE_AT["project_out"]:
                            project_out(j - 1)
                        if n == PE_AT["router_t"]:
                            router_t(j - 1)
                        if n == PE_AT["router"]:
                            router(j - 1)
                        if n == PE_AT["experts_t"]:
                            experts_t(j - 1, j + 2 if has_a else PAIRS)
                    if first(j):
                        for q in range(HR):
                            if n == PE_AT["bias_1"][q]:
                                bias_product(q)
                    if has_a:
                        if n == PE_AT["input_t"]:
                            input_t(j + 1)
                        if n == PE_AT["convolve"]:
                            convolve(j + 1)
                        if n == PE_AT["project_in"]:
                            project_in(j + 1)
                        if n == PE_AT["conv_t"]:
                            conv_t(j + 1)
                        if n == PE_AT["offsets"]:
                            offsets(j + 1)
                    if has_d:
                        for unit in range(2 * E):
                            if n == PE_AT["expert_in"][unit]:
                                expert_in(j - 1, unit)
                            if n == PE_AT["expert_out"][unit]:
                                expert_out(j - 1, unit, j + 2 if has_a else PAIRS)
                        for i in range(2):
                            if n == PE_AT["outputs_t"][i]:
                                outputs_t(j - 1, i)

            input_t(0)
            pe.wait_ge(s_dwd, 1)
            convolve(0)
            project_in(0)
            conv_t(0)
            pe.wait_ge(s_zero, 2)
            offsets(0)
            body(0, True, False)
            pe.wait_ge(s_w1, 1)
            with pe.Fori(1, PAIRS - 1) as j:
                body(j, True, True)
            body(PAIRS - 1, False, True)
            gather(PAIRS - 1, TP * NG - 1)
            samples_t(PAIRS - 1)
            project_out(PAIRS - 1)
            router_t(PAIRS - 1)
            router(PAIRS - 1)
            experts_t(PAIRS - 1, PAIRS)
            for i in range(2):
                for n in range(E + 2):
                    if n < E:
                        expert_in(PAIRS - 1, i * E + n)
                    if n >= 2:
                        expert_out(PAIRS - 1, i * E + n - 2, PAIRS)
                outputs_t(PAIRS - 1, i)


def layout(inputs):
    import numpy as np
    f = lambda n: np.ascontiguousarray(inputs[n])
    c = lambda n: f("L0_conv_" + n)
    m = lambda n: f("L0_ffn_" + n)
    with_bias = lambda w, b: np.concatenate([w, b[None, :]], 0)
    lnb = np.zeros((C, E, C + 1), np.float32)
    lnb[:, :, C] = m("ln_b").T
    return {
        "x": f("x"),
        "affine": np.concatenate([with_bias(c("w_in"), c("b_in")), with_bias(c("w_out"), c("b_out")),
                                  with_bias(c("w_off"), c("b_off")), with_bias(c("w_mask"), c("b_mask")),
                                  with_bias(m("Wr"), m("br"))], 1),
        "taps": c("dw_kernel").reshape(1, K2 * C),
        "biases": np.concatenate([c("dw_bias"), c("b_in")]).reshape(1, 2 * C),
        "vectors": np.concatenate([c("ln_gamma")[:, None], c("ln_beta")[:, None], m("ln_g").T, lnb.reshape(C, -1)], 1),
        "W1": m("W1").transpose(1, 0, 2).reshape(C, E * HID),
        "b1": m("b1").reshape(1, E * HID),
        "W2": m("W2").reshape(E * HC, P, C).transpose(1, 0, 2).reshape(P, E * HC * C),
        "b2": m("b2").reshape(1, E * C),
        "table": shape_table(),
    }


def shape_table():
    import numpy as np
    tab = np.zeros((P, NCONST), np.float32)
    put = lambda name, a: tab.__setitem__((slice(None), slice(*CI[name])), a)
    p = np.arange(P)[:, None]
    k = np.arange(K2)
    tap = lambda a: np.broadcast_to(a[:, None, :, None], (P, Q, K2, 2)).reshape(P, S)
    put("ident", np.eye(P))
    put("ubase", tap(p % W + k % 3 - 1))
    put("vbase", np.concatenate([tap(h * (H // 2) + p // W + k // 3 - 1) for h in range(2)], 1))
    put("pix", np.arange(H))
    put("loc", np.arange(LOC) - 1)
    put("thr", 4 * np.arange(1, CELLS) - 1)
    put("before", (np.arange(E)[None, :] < np.arange(E)[:, None]).reshape(1, -1))
    put("mhalf", -0.5)
    return tab


def kernel(**inputs):
    import numpy as _np
    import concourse.bacc as _bacc
    from concourse import mybir as _mybir
    from concourse.bass_utils import run_bass_kernel_spmd as _run

    nc = _bacc.Bacc("TRN2", target_bir_lowering=False, num_devices=1)
    arrays, args = {}, []
    for name, a in layout(inputs).items():
        a = _np.ascontiguousarray(a)
        arrays[f"in_{name}"] = a
        args.append(nc.dram_tensor(f"in_{name}", a.shape, _mybir.dt.from_np(a.dtype), kind="ExternalInput").ap())
    args.append(nc.dram_tensor("out_dram", (B, H, W, C), F32, kind="ExternalOutput").ap())
    build(nc, *args)
    r = _run(nc, [arrays], core_ids=[0])
    return r.results[0]["out_dram"]
```
